# Optimizing a Trainium2 kernel written in Bass

```python
import numpy as np
import jax
import jax.numpy as jnp

def _softmax(x, axis=-1):
    return jax.nn.softmax(x, axis=axis)

def _gelu(x):
    return jax.nn.gelu(x, approximate=True)

def _silu(x):
    return jax.nn.silu(x)

def _sigmoid(x):
    return jax.nn.sigmoid(x)

def _layernorm(x, axis=-1, eps=1e-05):
    m = jnp.mean(x, axis=axis, keepdims=True)
    v = jnp.var(x, axis=axis, keepdims=True)
    return (x - m) / jnp.sqrt(v + eps)

def _scatter_add(tgt, idx, src, axis=0):
    return tgt.at[idx].add(src)

def _segment_sum(src, seg, n):
    return jax.ops.segment_sum(src, seg, n)
kernel_name = 'mk_xattn_ffn_d2_seqx_r4_34813a'

def setup_inputs(seed: int=0):
    np.random.seed(seed)
    _w = jnp.asarray

    def _rec_inputs():
        import jax
        import jax.numpy as jnp
        _rk = jax.random.key(seed)
        x = -7.109e-05 + 0.9999 * jax.random.normal(jax.random.fold_in(_rk, 1), (4, 512, 512), jnp.float32)
        _lenS = 512 - jax.random.randint(jax.random.fold_in(_rk, 7), (4,), 0, max(1, 512 // 4) + 1, jnp.int32)
        _lenS2 = 512 - jax.random.randint(jax.random.fold_in(_rk, 8), (4,), 0, max(1, 512 // 4) + 1, jnp.int32)
        _ctx_512P = jax.random.normal(jax.random.fold_in(_rk, 11), (4, 16, 128), jnp.float32)
        _ctx_512c = jax.random.dirichlet(jax.random.fold_in(_rk, 511), 0.3 * jnp.ones((16,), jnp.float32), (4, 512))
        _ctx_512t = jnp.einsum('bsk,bkd->bsd', _ctx_512c, _ctx_512P)
        _ctx_512t = _ctx_512t * jax.lax.rsqrt(jnp.mean(jnp.square(_ctx_512t)) + 1e-12) * 0.953939
        ctx_512 = 2.81802e-05 + 1.00001 * (_ctx_512t + 0.3 * jax.random.normal(jax.random.fold_in(_rk, 611), (4, 512, 128), jnp.float32))
        return (x, ctx_512)
    x, ctx_512 = _rec_inputs()

    def _L0_xattn_setup():
        import jax, jax.numpy as jnp
        import numpy as np
        EPS = 1e-06
        IMAGE_DIMS = 512
        key = jax.random.key(seed)
        k1, k2, k3 = jax.random.split(key, 3)
        B, I, J, D = (16, 512, 512, 128)
        p = jax.random.normal(k1, (B, I, J), dtype=jnp.float32)
        k_v = jax.random.normal(k2, (B, J, D), dtype=jnp.float32)
        W_k = jax.random.normal(k3, (D, D), dtype=jnp.float32) * (1.0 / np.sqrt(D))
        b_k = jnp.zeros((D,), dtype=jnp.float32)
        ln_gamma = jnp.ones((J,), dtype=jnp.float32)
        ln_beta = jnp.zeros((J,), dtype=jnp.float32)
        return {'p': p, 'k_v': k_v, 'W_k': W_k, 'b_k': b_k, 'ln_gamma': ln_gamma, 'ln_beta': ln_beta}
    _L0_xattn_all = _L0_xattn_setup()
    _L0_xattn_in = {k: v for k, v in _L0_xattn_all.items() if k in ('W_k', 'b_k', 'ln_gamma', 'ln_beta')}
    del _L0_xattn_all

    def _L0_ffn_setup():
        import jax, jax.numpy as jnp
        import numpy as np
        EPS = 1e-05

        def fwht(x):
            orig_shape = x.shape
            n = orig_shape[-1]
            x = x.reshape(-1, n)
            h = 1
            while h < n:
                x = x.reshape(-1, n // (2 * h), 2, h)
                a, b = (x[:, :, 0, :], x[:, :, 1, :])
                x = jnp.stack([a + b, a - b], axis=2).reshape(-1, n)
                h *= 2
            return (x * (1.0 / np.sqrt(n))).reshape(orig_shape)

        def act_quant(x):
            scale = 127.0 / jnp.clip(jnp.max(jnp.abs(x), axis=-1, keepdims=True), EPS)
            q = jnp.clip(jnp.round(x * scale), -128.0, 127.0) / scale
            return x + jax.lax.stop_gradient(q - x)

        def weight_quant(w):
            scale = jnp.clip(jnp.mean(jnp.abs(w)), EPS)
            q = jnp.clip(jnp.round(w / scale), -1.0, 1.0) * scale
            return w + jax.lax.stop_gradient(q - w)

        def h_bitlinear(x, w):
            xq = act_quant(fwht(x))
            wq = weight_quant(w)
            return jnp.einsum('bsh,oh->bso', xq, wq)
        key = jax.random.key(seed)
        k1, k2, k3, k4 = jax.random.split(key, 4)
        H, I = (512, 2048)
        B, S = (2, 512)
        hidden_states = jax.random.normal(k1, (B, S, H), dtype=jnp.float32)
        w_gate = jax.random.normal(k2, (I, H), dtype=jnp.float32) * 0.02
        w_up = jax.random.normal(k3, (I, H), dtype=jnp.float32) * 0.02
        w_down = jax.random.normal(k4, (H, I), dtype=jnp.float32) * 0.02
        return {'hidden_states': hidden_states, 'w_gate': w_gate, 'w_up': w_up, 'w_down': w_down}
    _L0_ffn_all = _L0_ffn_setup()
    _L0_ffn_in = {k: v for k, v in _L0_ffn_all.items() if k in ('w_gate', 'w_up', 'w_down')}
    del _L0_ffn_all

    def _L1_xattn_setup():
        import jax, jax.numpy as jnp
        import numpy as np
        import math
        NUM_Q_HEADS = 32
        NUM_KV_HEADS = 8
        key = jax.random.key(seed)
        k1, k2, k3 = jax.random.split(key, 3)
        B, S, E = (2, 512, 512)
        kv_E = NUM_KV_HEADS * (E // NUM_Q_HEADS)
        q = jax.random.normal(k1, (B, S, E), dtype=jnp.float32)
        k = jax.random.normal(k2, (B, S, kv_E), dtype=jnp.float32)
        v = jax.random.normal(k3, (B, S, kv_E), dtype=jnp.float32)
        return {'q': q, 'k': k, 'v': v}
    _L1_xattn_all = _L1_xattn_setup()
    _L1_xattn_in = {k: v for k, v in _L1_xattn_all.items() if k in ()}
    del _L1_xattn_all

    def _L1_ffn_setup():
        import jax, jax.numpy as jnp
        import numpy as np
        B, S, D, M, E, K = (4, 512, 512, 1024, 8, 2)

        def _routed_moe(x, gate_w, w0, w1, wo):
            T = x.shape[0]
            logits = jnp.einsum('td,de->te', x, gate_w)
            top_logits, top_idx = jax.lax.top_k(logits, K)
            top_w = jax.nn.softmax(top_logits, axis=-1)
            cw = jnp.zeros((T, E), dtype=x.dtype).at[jnp.arange(T)[:, None], top_idx].add(top_w)
            out = jnp.zeros_like(x)
            for e in range(E):
                h = jax.nn.silu(x @ w0[e]) * (x @ w1[e])
                out = out + cw[:, e:e + 1] * (h @ wo[e])
            return out
        key = jax.random.key(seed)
        ks = jax.random.split(key, 5)
        inputs = jax.random.normal(ks[0], (B, S, D), dtype=jnp.float32)
        gate_w = jax.random.normal(ks[1], (D, E), dtype=jnp.float32) * D ** (-0.5)
        w0 = jax.random.normal(ks[2], (E, D, M), dtype=jnp.float32) * D ** (-0.5)
        w1 = jax.random.normal(ks[3], (E, D, M), dtype=jnp.float32) * D ** (-0.5)
        wo = jax.random.normal(ks[4], (E, M, D), dtype=jnp.float32) * M ** (-0.5)
        decoder_segment_ids = jax.random.randint(jax.random.fold_in(key, 1), (B, S), 0, 2).astype(jnp.int32)
        decoder_positions = jnp.tile(jnp.arange(S, dtype=jnp.int32)[None, :], (B, 1))
        return {'inputs': inputs, 'gate_w': gate_w, 'w0': w0, 'w1': w1, 'wo': wo, 'decoder_segment_ids': decoder_segment_ids, 'decoder_positions': decoder_positions}
    _L1_ffn_all = _L1_ffn_setup()
    _L1_ffn_in = {k: v for k, v in _L1_ffn_all.items() if k in ('gate_w', 'w0', 'w1', 'wo', 'decoder_segment_ids', 'decoder_positions')}
    del _L1_ffn_all
    return {'x': x, 'ctx_512': ctx_512, 'L0_xattn_W_k': _L0_xattn_in['W_k'], 'L0_xattn_b_k': _L0_xattn_in['b_k'], 'L0_xattn_ln_gamma': _L0_xattn_in['ln_gamma'], 'L0_xattn_ln_beta': _L0_xattn_in['ln_beta'], 'L0_ffn_w_gate': _L0_ffn_in['w_gate'], 'L0_ffn_w_up': _L0_ffn_in['w_up'], 'L0_ffn_w_down': _L0_ffn_in['w_down'], 'L1_ffn_gate_w': _L1_ffn_in['gate_w'], 'L1_ffn_w0': _L1_ffn_in['w0'], 'L1_ffn_w1': _L1_ffn_in['w1'], 'L1_ffn_wo': _L1_ffn_in['wo'], 'L1_ffn_decoder_segment_ids': _L1_ffn_in['decoder_segment_ids'], 'L1_ffn_decoder_positions': _L1_ffn_in['decoder_positions']}

def reference(x, ctx_512, L0_xattn_W_k, L0_xattn_b_k, L0_xattn_ln_gamma, L0_xattn_ln_beta, L0_ffn_w_gate, L0_ffn_w_up, L0_ffn_w_down, L1_ffn_gate_w, L1_ffn_w0, L1_ffn_w1, L1_ffn_wo, L1_ffn_decoder_segment_ids, L1_ffn_decoder_positions):
    import jax
    import jax.numpy as jnp

    def _L0_xattn_ref(p, k_v, W_k, b_k, ln_gamma, ln_beta):
        import jax, jax.numpy as jnp
        import numpy as np
        EPS = 1e-06
        IMAGE_DIMS = 512
        kv = k_v @ W_k.T + b_k
        out = jnp.einsum('bij,bjd->bid', p, kv)
        scale = IMAGE_DIMS ** (-0.5)
        sim = jnp.einsum('bid,bjd->bij', out, kv) * scale
        mu = jnp.mean(sim, axis=-1, keepdims=True)
        var = jnp.var(sim, axis=-1, keepdims=True)
        sim = (sim - mu) * jax.lax.rsqrt(var + EPS) * ln_gamma + ln_beta
        attn = jax.nn.softmax(sim, axis=-1)
        return attn

    def _L0_ffn_ref(hidden_states, w_gate, w_up, w_down):
        import jax, jax.numpy as jnp
        import numpy as np
        EPS = 1e-05

        def fwht(x):
            orig_shape = x.shape
            n = orig_shape[-1]
            x = x.reshape(-1, n)
            h = 1
            while h < n:
                x = x.reshape(-1, n // (2 * h), 2, h)
                a, b = (x[:, :, 0, :], x[:, :, 1, :])
                x = jnp.stack([a + b, a - b], axis=2).reshape(-1, n)
                h *= 2
            return (x * (1.0 / np.sqrt(n))).reshape(orig_shape)

        def act_quant(x):
            scale = 127.0 / jnp.clip(jnp.max(jnp.abs(x), axis=-1, keepdims=True), EPS)
            q = jnp.clip(jnp.round(x * scale), -128.0, 127.0) / scale
            return x + jax.lax.stop_gradient(q - x)

        def weight_quant(w):
            scale = jnp.clip(jnp.mean(jnp.abs(w)), EPS)
            q = jnp.clip(jnp.round(w / scale), -1.0, 1.0) * scale
            return w + jax.lax.stop_gradient(q - w)

        def h_bitlinear(x, w):
            xq = act_quant(fwht(x))
            wq = weight_quant(w)
            return jnp.einsum('bsh,oh->bso', xq, wq)
        gate = h_bitlinear(hidden_states, w_gate)
        up = h_bitlinear(hidden_states, w_up)
        return h_bitlinear(jax.nn.silu(gate) * up, w_down)

    def _L1_xattn_ref(q, k, v):
        import jax, jax.numpy as jnp
        import numpy as np
        import math
        NUM_Q_HEADS = 32
        NUM_KV_HEADS = 8
        B, S, E = q.shape
        H, KV = (NUM_Q_HEADS, NUM_KV_HEADS)
        D = E // H
        G = H // KV
        scale = math.sqrt(D)
        qh = q.reshape(B, S, KV, G, D).transpose(0, 2, 3, 1, 4)
        kh = k.reshape(B, S, KV, D).transpose(0, 2, 1, 3)
        vh = v.reshape(B, S, KV, D).transpose(0, 2, 1, 3)
        scores = jnp.einsum('bkgsd,bktd->bkgst', qh, kh) / scale
        weights = jax.nn.softmax(scores, axis=-1)
        out = jnp.einsum('bkgst,bktd->bkgsd', weights, vh)
        return out.transpose(0, 3, 1, 2, 4).reshape(B, S, E)

    def _L1_ffn_ref(inputs, gate_w, w0, w1, wo, decoder_segment_ids, decoder_positions):
        import jax, jax.numpy as jnp
        import numpy as np
        B, S, D, M, E, K = (4, 512, 512, 1024, 8, 2)

        def _routed_moe(x, gate_w, w0, w1, wo):
            T = x.shape[0]
            logits = jnp.einsum('td,de->te', x, gate_w)
            top_logits, top_idx = jax.lax.top_k(logits, K)
            top_w = jax.nn.softmax(top_logits, axis=-1)
            cw = jnp.zeros((T, E), dtype=x.dtype).at[jnp.arange(T)[:, None], top_idx].add(top_w)
            out = jnp.zeros_like(x)
            for e in range(E):
                h = jax.nn.silu(x @ w0[e]) * (x @ w1[e])
                out = out + cw[:, e:e + 1] * (h @ wo[e])
            return out
        b, s, d = inputs.shape
        x = inputs.reshape(b * s, d)
        out = _routed_moe(x, gate_w, w0, w1, wo)
        return out.reshape(b, s, d)
    x = x + _L0_xattn_ref(_layernorm(x, axis=-1), ctx_512, L0_xattn_W_k, L0_xattn_b_k, L0_xattn_ln_gamma, L0_xattn_ln_beta)
    x = x + _L0_ffn_ref(_layernorm(x, axis=-1), L0_ffn_w_gate, L0_ffn_w_up, L0_ffn_w_down)
    x = x + _L1_xattn_ref(_layernorm(x, axis=-1), ctx_512, ctx_512)
    x = x + _L1_ffn_ref(_layernorm(x, axis=-1), L1_ffn_gate_w, L1_ffn_w0, L1_ffn_w1, L1_ffn_wo, L1_ffn_decoder_segment_ids, L1_ffn_decoder_positions)
    return x

_drawn_inputs = setup_inputs


def setup_inputs(seed=0):
    import zlib

    import numpy as np

    out = dict(_drawn_inputs(seed))
    spreads = {'L0_xattn_b_k': (0.0, 2.0),
     'L0_xattn_ln_gamma': (1.0, 0.6),
     'L0_xattn_ln_beta': (0.0, 2.0)}
    factors = {'L0_xattn_W_k': 4.288}
    for name, (base, spread) in spreads.items():
        noise = np.random.default_rng([zlib.crc32(name.encode()), seed]).standard_normal(out[name].shape)
        drawn = base * np.exp(spread * noise) if base else spread * noise
        out[name] = jnp.asarray(drawn.astype(out[name].dtype))
    for name, factor in factors.items():
        out[name] = (out[name] * factor).astype(out[name].dtype)
    return out
```

```python
import math
from contextlib import ExitStack

import concourse.bass as bass
import numpy as np
from concourse import mybir

F32 = mybir.dt.float32
F32R = mybir.dt.float32r
BF16 = mybir.dt.bfloat16
I32 = mybir.dt.int32
ALU = mybir.AluOpType
ACT = mybir.ActivationFunctionType
AX = mybir.AxisListType

P = 128
BATCH, SEQ, D = 4, 512, 512
TILES = BATCH * SEQ // P
ST = SEQ // P
DC = D // P
CTX = 128
FF = 2048
FC = FF // P
HEADS, KVH, HD = 32, 8, 16
GROUP = HEADS // KVH
EXPERTS, MOE = 8, 1024
MTILES = 2 * TILES + EXPERTS - 1
ROWS = MTILES * P
EPS_SCORE, EPS_LN, EPS_Q = 1e-6, 1e-5, 1e-5
SCORE_SCALE = D ** -0.5
MAGIC = 1.5 * 2.0 ** 23
HAD_D, HAD_FF = 1.0 / math.sqrt(D), 1.0 / math.sqrt(FF)


class Count:

    def __init__(self, eng, sem, carrier=None):
        self.eng, self.sem, self.n, self.loops, self.carrier = eng, sem, 0, [], carrier

    def enter(self, i, per):
        self.loops.append((i, per, self.n))

    def leave(self, times):
        _, per, before = self.loops.pop()
        assert self.n - before == per, (self.n - before, per)
        self.n = before + per * times

    def inc(self, instruction):
        instruction.then_inc(self.sem, 1)
        self.n += 1

    def wait(self):
        value = self.n
        for i, per, _ in self.loops:
            value = value + i * per
        self.eng.wait_ge(self.sem, value)
        if self.carrier is not None:
            self.eng.sem_inc(self.carrier, 1)

    def step(self, instruction):
        self.inc(instruction)
        self.wait()


class Map:

    def __init__(self, nc, start, end):
        self.nc, self.start, self.at, self.end = nc, start, start, end

    def again(self):
        self.at = self.start

    def tile(self, name, shape, dtype=F32):
        size = int(np.prod(shape[1:])) * mybir.dt.size(dtype)
        t = self.nc.alloc_sbuf_tensor_at(name, list(shape), dtype, offset=self.at)
        self.at += (size + 31) // 32 * 32
        assert self.at <= self.end, (name, self.at - self.end)
        return t


def network(nc, x, ctx_512, w_k, b_k, ln_gamma, ln_beta, w_gate, w_up, w_down, gate_w, w0, w1, wo,
            c_ident, c_hadamard, c_before, c_routing, out):
    with ExitStack() as stack:
        def sem(name):
            return stack.enter_context(nc.semaphore(name))

        first = (nc.sbuf_base + 63) // 64 * 64
        keep = Map(nc, first, first + 37 * 1024)
        X = keep.tile("x_tiles", [P, TILES * D])
        ident = keep.tile("ident", [P, P])
        ident_b = keep.tile("ident_bf16", [P, P], BF16)
        st6 = keep.tile("ln_stats6", [P, ST * 6])
        mv = keep.tile("ln_mean_var", [P, ST * 2])
        var_eps = keep.tile("ln_var_eps", [P, ST])
        rstd = keep.tile("ln_rstd", [P, ST])
        half_neg = keep.tile("minus_half", [P, ST])
        magic = keep.tile("magic", [P, 1])
        ones = keep.tile("ones", [P, P])
        silu_first = keep.tile("silu_first", [P, 1])
        abs_sum = keep.tile("weight_abs_sum", [P, 3])
        w_mean = keep.tile("weight_scale", [P, 3])
        w_thr = keep.tile("weight_threshold", [P, 3])
        w_nthr = keep.tile("weight_neg_threshold", [P, 3])
        st6_all = keep.tile("stats6_all", [P, TILES * 6])
        mv_all = keep.tile("mean_var_all", [P, TILES * 2])
        ve_all = keep.tile("var_eps_all", [P, TILES])
        rstd_all = keep.tile("rstd_all", [P, TILES])
        half_neg_all = keep.tile("minus_half_all", [P, TILES])
        big = Map(nc, keep.end, keep.end + 112 * 1024)
        small = Map(nc, big.end, nc.sbuf_usable_end)
        first_small = small.start

        raw = [big.tile(f"raw_weight{i}", [P, FF * D // P]) for i in range(2)]
        wgu_t = [big.tile(f"{n}_ternary_t", [P, DC * FF], BF16) for n in ("gate", "up")]
        wd_t = big.tile("down_ternary_t", [P, FC * D], BF16)
        big.again()
        Y = big.tile("inner_t", [P, FC * SEQ])
        Z = big.tile("inner_half_rotated_t", [P, FC * SEQ])
        big.again()
        Y_lo = big.tile("inner_rotated_t_second", [P, FC * SEQ], F32R)
        Z_hi = big.tile("inner_rotated_t_first", [P, FC * SEQ], F32R)
        big.again()
        h_lo = big.tile("normed_tiles_t_second", [P, ST * D], F32R)

        neg = [small.tile(f"below_threshold{i}", [P, 512], BF16) for i in range(2)]
        tern = [small.tile(f"ternary_rows{i}", [P, 512], BF16) for i in range(2)]
        small.start = small.at

        a_p = small.tile("normed_tokens", [P, ST * D])
        a_pt = small.tile("normed_t", [P, DC * SEQ])
        ctx_t = small.tile("context_t", [CTX, BATCH * SEQ])
        kv_t = small.tile("kv_t", [CTX, SEQ])
        kv = small.tile("kv_tokens", [P, ST * CTX])
        o_t = small.tile("pair_product_t", [CTX, SEQ])
        gamma = small.tile("gamma_rows", [P, SEQ])
        beta = small.tile("beta_rows", [P, SEQ])
        wk_sb = small.tile("w_k", [CTX, CTX])
        wk_t = small.tile("w_k_t", [CTX, CTX])
        bk_col = small.tile("b_k_column", [CTX, 1])
        a_e = small.tile("score_exp", [P, ST * SEQ])
        a_mx = small.tile("score_neg_max", [P, ST])
        a_sum = small.tile("score_exp_sum", [P, ST])
        a_rs = small.tile("score_exp_rsum", [P, ST])
        keep_small = small.at
        a_z = small.tile("score_normed", [P, ST * SEQ])
        small.at = keep_small
        ctx_raw = small.tile("context_tokens", [P, TILES * CTX])

        small.again()
        h_b = small.tile("normed_or_scaled_tokens", [P, ST * D])
        here = small.at
        h_hi = small.tile("normed_tiles_t_first", [P, ST * D], F32R)
        small.at = here
        z_s = [small.tile("inner_rotated_rows0", [P, FF])]
        had = small.tile("hadamard", [P, DC * D], F32R)
        diag = small.tile("token_scale_diagonals", [P, ST * P])
        scale_rows = small.tile("token_scale_rows", [P, SEQ])
        q_b = small.tile("quantised_tokens", [P, FF], BF16)
        q_t = small.tile("quantised_t", [P, DC * SEQ], BF16)
        g_s = [small.tile(f"gate_scaled{i}", [P, SEQ]) for i in range(2)]
        g_silu = [small.tile(f"gate_silu{i}", [P, SEQ]) for i in range(2)]
        z_s.append(Map(nc, small.at - 4 * 4 * SEQ, small.at).tile("inner_rotated_rows1", [P, FF]))
        q2_t = small.tile("inner_quantised_t", [P, FC * P], BF16)
        am = small.tile("abs_max", [P, ST])
        am_c = small.tile("abs_max_clipped", [P, ST])
        am_r = small.tile("abs_max_reciprocal", [P, ST])
        fac = small.tile("quantise_factor", [P, ST])
        tok_scale = small.tile("token_scale", [P, ST])
        inner_scale = small.tile("inner_scale", [P, ST])
        am2 = small.tile("inner_abs_max", [P, ST])
        am2_c = small.tile("inner_abs_max_clipped", [P, ST])
        am2_r = small.tile("inner_abs_max_reciprocal", [P, ST])
        fac2 = small.tile("inner_quantise_factor", [P, ST])
        deq = small.tile("inner_dequantise", [P, ST])

        small.start = first_small
        small.again()
        tail = Map(nc, big.end - 16 * 1024, big.end)
        ctx_c = tail.tile("context_tokens_again", [P, TILES * CTX])
        q_f = [small.tile(f"query_unit{i}", [P, ST * GROUP * HD]) for i in range(2)]
        q_s = [small.tile(f"query_parts{i}", [P, ST * GROUP * 64], F32R) for i in range(4)]
        k_s = [small.tile(f"key_parts_twice{i}", [P, ST * 2 * 64], F32R) for i in range(2)]
        v_u = [(keep if i < 4 else small).tile(f"value_and_one{i}", [P, ST * 32]) for i in range(8)]
        k_lo = [small.tile(f"key_t_first{i}", [P, SEQ], F32R) for i in range(4)]
        k_hi = [small.tile(f"key_t_second{i}", [P, SEQ], F32R) for i in range(4)]
        q_m = [small.tile(f"query_t_for_max{p}", [P, SEQ], F32R) for p in range(2)]
        q_e = [[small.tile(f"query_t_for_exp{i}{p}", [P, SEQ], F32R) for p in range(2)] for i in range(2)]
        prob = [tail.tile(f"probabilities{i}", [P, 2 * SEQ]) for i in range(2)]
        att_t = small.tile("attended_t", [P, SEQ])
        neg_max = [small.tile(f"neg_max{i}", [P, ST * GROUP]) for i in range(2)]
        att_r = small.tile("attended_rsum", [P, ST * GROUP])
        att_n = small.tile("attended_normed", [P, ST * GROUP * HD])

        zero_rows = small.tile("zero_rows", [P, D])

        big.again()
        EXPERT_COLS = 3 * DC * MOE
        w_all = big.tile("expert_weights", [P, 2 * EXPERT_COLS])
        tail = Map(nc, big.at, big.end)
        x_in = [tail.tile(f"sorted_tokens{i}", [P, D]) for i in range(2)]
        x_t = [tail.tile(f"sorted_tokens_t{i}", [P, D]) for i in range(2)]
        g_silu_d = [tail.tile(f"expert_gate_silu{i}", [P, 512]) for i in range(2)]
        y_out = [tail.tile(f"expert_out{i}", [P, D]) for i in range(2)]
        small.again()
        xn = small.tile("normed_all", [P, TILES * D])
        xn_t = [small.tile(f"normed_all_t{i}", [P, D]) for i in range(2)]
        h_d = small.tile("expert_inner", [P, MOE])
        h_dt = small.tile("expert_inner_t", [P, MOE])
        early = Map(nc, small.at - 2 * 4 * MOE, small.at)
        past_end = early.tile("past_end", [1, MTILES * EXPERTS])
        mt = {n: early.tile(f"tile_{n}", [1, MTILES]) for n in ("expert", "half", "half_up", "parity", "first")}
        mt_i = {n: early.tile(f"tilei_{n}", [1, MTILES], I32) for n in ("expert", "next", "half", "half_up")}
        gw = small.tile("router_weights", [P, DC * EXPERTS])
        before = small.tile("strictly_before", [P, P])
        num_e = small.tile("expert_numbers", [P, TILES * EXPERTS])
        num_tile = small.tile("tile_numbers", [1, MTILES * EXPERTS])
        lg = small.tile("logits", [P, TILES * EXPERTS])
        top = small.tile("logits_sorted", [P, TILES * EXPERTS])
        chosen = [small.tile(f"chosen{k}", [P, TILES * EXPERTS]) for k in range(2)]
        both = small.tile("chosen_either", [P, TILES * EXPERTS])
        running = small.tile("running_counts", [P, (TILES + 1) * EXPERTS])
        slot_e = small.tile("slot_by_expert", [P, TILES * EXPERTS])
        picked = [small.tile(f"slot_picked{k}", [P, TILES * EXPERTS]) for k in range(2)]
        slot_f = [small.tile(f"slot_f32_{k}", [P, TILES]) for k in range(2)]
        slot = [small.tile(f"slot{k}", [P, TILES], I32) for k in range(2)]
        gap = small.tile("logit_gap", [P, TILES])
        gap_e = small.tile("logit_gap_exp", [P, TILES])
        gap_1 = small.tile("softmax_sum", [P, TILES])
        top_w = [small.tile(f"top_weight{k}", [P, TILES]) for k in range(2)]
        row8 = {n: small.tile(f"experts_{n}", [P, EXPERTS]) for n in ("tiles", "end", "first")}
        row8_i = {n: small.tile(f"experts_{n}_int", [P, EXPERTS], I32) for n in ("count", "tiles", "wait")}
        last_free = small.tile("first_unused_slot", [1, 1])
        plan = small.tile("tile_plan", [1, 3 * MTILES], I32)
        sorted_x = nc.dram_tensor("sorted_x", (ROWS, D), F32, kind="Internal").ap()
        sorted_y = nc.dram_tensor("sorted_y", (ROWS, D), F32, kind="Internal").ap()

        psum = stack.enter_context(nc.psum_tensor("psum", [P, 8 * 512], F32))
        bank = [psum[:, 512 * i:512 * i + 512] for i in range(8)]
        bank_b = [b.bitcast(BF16) for b in bank]

        def tiles(buf, i, n=1, width=D):
            return buf[:, bass.ds(i * width, n * width)]

        ld_const, ld_x, ld_ctx = sem("ld_const"), sem("ld_x"), sem("ld_ctx")
        ld_raw = [sem("ld_raw0"), sem("ld_raw1"), sem("ld_raw2")]
        stored = sem("stored")
        pool_const, dve_const = sem("pool_const"), sem("dve_const")
        dve_step, act_step, pool_step = sem("dve_step"), sem("act_step"), sem("pool_step")
        ctx_t_ps, ctx_t_sb = sem("ctx_t_ps"), sem("ctx_t_sb")
        ln_var, ln_rstd = sem("ln_var"), sem("ln_rstd")
        a_normed, a_trans, a_trans_sb = sem("a_normed"), sem("a_trans"), sem("a_trans_sb")
        a_kvt, a_kvt_sb, a_kv, a_kv_sb = sem("a_kvt"), sem("a_kvt_sb"), sem("a_kv"), sem("a_kv_sb")
        a_out, a_out_sb, a_sim, a_simz = sem("a_out"), sem("a_out_sb"), sem("a_sim"), sem("a_simz")
        a_zg, a_neg, a_exp, a_done = sem("a_zg"), sem("a_neg"), sem("a_exp"), sem("a_done")

        w_abs, w_tot, w_mean_r = sem("w_abs"), sem("w_tot"), sem("w_mean_r")
        w_tern, w_tp, w_evac = sem("w_tern"), sem("w_tp"), sem("w_evac")
        ld_had, had_ready = sem("ld_had"), sem("had_ready")
        b_normed, b_trans, b_trans_sb, b_fw, b_fac = sem("b_normed"), sem("b_trans"), sem("b_trans_sb"), sem("b_fw"), sem("b_fac")
        b_tq, b_q, b_qt, b_qts = sem("b_tq"), sem("b_q"), sem("b_qt"), sem("b_qts")
        b_dg, b_sps, b_sbc = sem("b_dg"), sem("b_sps"), sem("b_sbc")
        b_gp, b_up, b_g, b_sl, b_y, b_rot = sem("b_gp"), sem("b_up"), sem("b_g"), sem("b_sl"), sem("b_y"), sem("b_rot")
        b_lo, b_half, b_zhi, b_zlo, b_zlo0, b_zc = sem("b_lo"), sem("b_half"), sem("b_zhi"), sem("b_zlo"), sem("b_zlo0"), sem("b_zc")
        b_z, b_fac2, b_tq2, b_q2, b_tr, b_q2ts, b_dn, b_x = (sem("b_z"), sem("b_fac2"), sem("b_tq2"), sem("b_q2"),
                                                             sem("b_tr"), sem("b_q2ts"), sem("b_dn"), sem("b_x"))

        ld_ctx2, c_const, c_var, c_rstd, c_prep = sem("ld_ctx2"), sem("c_const"), sem("c_var"), sem("c_rstd"), sem("c_prep")
        c_tqe, c_tk, c_tqm, c_to = sem("c_tqe"), sem("c_tk"), sem("c_tqm"), sem("c_to")
        c_eqe, c_ek, c_eqm, c_eo = sem("c_eqe"), sem("c_ek"), sem("c_eqm"), sem("c_eo")
        c_mx, c_red, c_m, c_s, c_e, c_pv, c_oe = (sem("c_mx"), sem("c_red"), sem("c_m"), sem("c_s"), sem("c_e"),
                                                  sem("c_pv"), sem("c_oe"))

        c_x, pool_waited = sem("c_x"), sem("pool_waited")
        ld_d, ld_w = sem("ld_d"), [sem("ld_w_even"), sem("ld_w_odd")]
        d_xn, d_tr, d_trs, d_lg, d_both, d_rank, d_slot, d_gap, d_gap_e, d_plan = (
            sem("d_xn"), sem("d_tr"), sem("d_trs"), sem("d_lg"), sem("d_both"), sem("d_rank"), sem("d_slot"),
            sem("d_gap"), sem("d_gap_e"), sem("d_plan"))
        d_sc, d_zf, d_zero = sem("d_sc"), sem("d_zf"), sem("d_zero")
        e_ld, e_st = [sem("e_ld0"), sem("e_ld1")], [sem("e_st0"), sem("e_st1")]
        e_xtr, e_xt, e_gu, e_silu, e_h, e_htr, e_ht0, e_ht1, e_wo, e_y = (
            sem("e_xtr"), sem("e_xt"), sem("e_gu"), sem("e_silu"), sem("e_h"), sem("e_htr"), sem("e_ht0"), sem("e_ht1"),
            sem("e_wo"), sem("e_y"))
        d_got = [sem(f"d_got{i}") for i in range(8)]
        d_out = sem("d_out")

        def tile_loop(eng, step):
            step(0, 0)
            step(1, 1)
            step(2, 0)
            with eng.Fori(1, (MTILES - 3) // 2) as r:
                step(2 * r + 1, 1)
                step(2 * r + 2, 0)
            step(MTILES - 2, 1)
            step(MTILES - 1, 0)

        def token_tile(buf, st):
            return buf[:].rearrange("p (c n) -> p c n", c=FC)[:, :, st * P:(st + 1) * P]

        def static(i):
            return isinstance(i, int)
        UNITS = BATCH * KVH
        PAIRS = 2 * ST

        def slots(eng, slot, count=None, per=0):
            def bounded(v):
                return 0 <= v < UNITS
            for u in range(-2, KVH):
                slot(u, u % KVH, bounded)
            with eng.Fori(1, BATCH - 1) as b:
                if count:
                    count.enter(b - 1, per)
                for j in range(KVH):
                    slot(b * KVH + j, j, lambda v: True)
                if count:
                    count.leave(BATCH - 2)
            for u in range(UNITS - KVH, UNITS + 2):
                slot(u, u % KVH, bounded)

        block = stack.enter_context(nc.Block())

        @block.sync
        def _(sp):
            sp.dma_start(ident[:], c_ident).then_inc(ld_const, 16)
            sp.dma_start(ctx_raw[:].rearrange("p (t c) -> p t c", c=CTX),
                         ctx_512.rearrange("b (t p) c -> p (b t) c", p=P)).then_inc(ld_ctx, 16)
            sp.dma_start(wk_sb[:], w_k).then_inc(ld_const, 16)
            sp.dma_start(bk_col[:], b_k.rearrange("(p a) -> p a", a=1)).then_inc(ld_const, 16)
            sp.dma_start(gamma[:], ln_gamma.partition_broadcast(P)).then_inc(ld_const, 16)
            sp.dma_start(beta[:], ln_beta.partition_broadcast(P)).then_inc(ld_const, 16)
            sp.dma_start(X[:].rearrange("p (t c) -> p t c", c=D),
                         x.rearrange("b (t p) c -> p (b t) c", p=P)).then_inc(ld_x, 16)
            sp.dma_start(raw[0][:].rearrange("p (t c) -> p t c", c=D),
                         w_gate.rearrange("(t p) c -> p t c", p=P)).then_inc(ld_raw[0], 16)
            sp.dma_start(raw[1][:].rearrange("p (t c) -> p t c", c=D),
                         w_up.rearrange("(t p) c -> p t c", p=P)).then_inc(ld_raw[1], 16)
            sp.wait_ge(a_done, BATCH * ST)
            sp.dma_start(h_b[:], c_hadamard).then_inc(ld_had, 16)
            sp.wait_ge(w_tern, FC)
            sp.wait_ge(w_abs, 1)
            sp.dma_start(raw[0][:].rearrange("p (t c) -> p t c", c=FF),
                         w_down.rearrange("(t p) c -> p t c", p=P)).then_inc(ld_raw[2], 16)
            sp.wait_ge(b_x, BATCH * ST)
            sp.dma_start(ctx_c[:].rearrange("p (t c) -> p t c", c=CTX),
                         ctx_512.rearrange("b (t p) c -> p (b t) c", p=P)).then_inc(ld_ctx2, 16)
            def load_expert(e):
                at = (e % 2) * EXPERT_COLS
                for i, w in enumerate((w0, w1)):
                    sp.dma_start(w_all[:, at + i * DC * MOE:at + (i + 1) * DC * MOE].rearrange("p (k m) -> p k m", k=DC),
                                 w[e, :, :].rearrange("(k p) m -> p k m", p=P)).then_inc(ld_w[e % 2], 16)
                sp.dma_start(w_all[:, at + 2 * DC * MOE:at + 3 * DC * MOE].rearrange("p (k m) -> p k m", k=MOE // P),
                             wo[e, :, :].rearrange("(k p) m -> p k m", p=P)).then_inc(ld_w[e % 2], 16)

            load_expert(0)
            load_expert(1)
            sp.wait_ge(d_zero, 1)
            sp.dma_start(sorted_x.rearrange("(t p) c -> p t c", p=P),
                         zero_rows[:].rearrange("p (t c) -> p t c", t=1).broadcast_to([P, MTILES, D])).then_inc(d_zf, 16)
            sp.wait_ge(c_x, UNITS)
            sp.dma_start(gw[:].rearrange("p (k e) -> p k e", k=DC), gate_w.rearrange("(k p) e -> p k e", p=P)).then_inc(ld_d, 16)
            sp.dma_start(before[:], c_before).then_inc(ld_d, 16)
            n = TILES * EXPERTS
            sp.dma_start(num_e[:], c_routing[0, 0:n].partition_broadcast(P)).then_inc(ld_d, 16)
            sp.dma_start(num_tile[:], c_routing[1:2, 0:MTILES * EXPERTS]).then_inc(ld_d, 16)
            sp.wait_ge(d_plan, 1)
            for e in range(2, EXPERTS):
                end = sp.value_load(row8_i["wait"][0:1, e - 2:e - 1], min_val=1, max_val=MTILES + 1)
                sp.wait_ge(e_wo, end)
                load_expert(e)
            for t in range(TILES):
                sp.wait_ge(d_out, 2 * t + 2)
                sp.dma_start(out[t // ST, (t % ST) * P:(t % ST + 1) * P, :], X[:, t * D:(t + 1) * D]).then_inc(stored, 16)
            sp.wait_ge(stored, TILES * 16)

        @block.gpsimd
        def _(pool):
            nc.gpsimd.memset(half_neg[:], -0.5).then_inc(pool_const, 1)
            nc.gpsimd.memset(ones[:], 1.0).then_inc(pool_const, 1)
            nc.gpsimd.memset(magic[:], MAGIC).then_inc(pool_const, 1)
            c = Count(pool, pool_step, pool_waited)

            def inverse_root(n):
                pool.wait_ge(ln_var, n)
                nc.gpsimd.tensor_tensor(rstd[:], var_eps[:], half_neg[:], ALU.pow).then_inc(ln_rstd, 1)

            def phase_a(b):
                inverse_root(2 * b + 1)
                inverse_root(2 * b + 2)
                for st in range(ST):
                    pool.wait_ge(a_simz, b * ST + st + 1)
                    z = a_z[:, st * SEQ:(st + 1) * SEQ]
                    c.step(nc.gpsimd.tensor_tensor(z, z, gamma[:], ALU.mult))
                    nc.gpsimd.tensor_tensor(z, z, beta[:], ALU.add).then_inc(a_zg, 1)

            def phase_b(b):
                for a in range(2):
                    with pool.Fori(0, 4) as i:
                        pool.wait_ge(b_y, 2 + b * FC + a * 8 + 2 * i + 2)
                        pool.sem_inc(pool_waited, 1)
                        y0, y1 = (Y[:, bass.ds((8 * a + i + 4 * h) * SEQ, SEQ)] for h in range(2))
                        nc.gpsimd.tensor_tensor(Z[:, bass.ds((8 * a + i) * SEQ, SEQ)], y0, y1, ALU.add).then_inc(b_half, 1)
                        nc.gpsimd.tensor_tensor(Z[:, bass.ds((8 * a + i + 4) * SEQ, SEQ)], y0, y1, ALU.subtract).then_inc(b_half, 1)
                for st in range(1, ST):
                    pool.wait_ge(b_zhi, b * ST + st + 1)
                    pool.sem_inc(pool_waited, 1)
                    nc.gpsimd.tensor_tensor(token_tile(Y_lo, st), token_tile(Y, st), token_tile(Z_hi, st),
                                            ALU.subtract).then_inc(b_zlo, 1)

            def phase_c(c):
                pool.wait_ge(b_x, BATCH * ST)
                for parts in q_s + k_s:
                    nc.gpsimd.memset(parts[:].bitcast(F32), 0.0).then_inc(c_const, 1)
                pool.wait_ge(c_const, 6)
                for v in v_u:
                    nc.gpsimd.memset(v[:], 0.0).then_inc(c_const, 1)
                pool.wait_ge(c_const, 14)
                for i in range(4):
                    nc.gpsimd.memset(k_lo[i][64:P, :].bitcast(F32), 0.0).then_inc(c_const, 1)
                    nc.gpsimd.memset(k_hi[i][0:64, :].bitcast(F32), 0.0).then_inc(c_const, 1)
                    pool.wait_ge(c_const, 16 + 2 * i)
                nc.gpsimd.memset(half_neg_all[:], -0.5).then_inc(c_const, 1)
                pool.wait_ge(c_const, 23)
                nc.gpsimd.memset(zero_rows[:], 0.0).then_inc(d_zero, 1)
                for i in range(2):
                    nc.gpsimd.memset(k_s[i][:].bitcast(F32).rearrange("p (t c) -> p t c", c=64)[:, :, 48:50], 1.0).then_inc(c_const, 1)
                for i in range(8):
                    nc.gpsimd.memset(v_u[i][:].rearrange("p (t c) -> p t c", c=32)[:, :, HD:HD + 1], 1.0).then_inc(c_const, 1)
                pool.wait_ge(c_const, 33)
                pool.wait_ge(c_var, 1)
                nc.gpsimd.tensor_tensor(rstd_all[:], ve_all[:], half_neg_all[:], ALU.pow).then_inc(c_rstd, 1)
                pool.wait_ge(c_rstd, 1)
                pool.wait_ge(ld_ctx2, 16)
                with pool.Fori(0, BATCH) as b:
                    c.enter(b, KVH * 7)
                    for j in range(KVH):
                        unit_parts(c, b, j)
                    c.leave(BATCH)

            def phase_d():
                pool.wait_ge(c_x, UNITS)
                pool.wait_ge(c_var, 2)
                nc.gpsimd.tensor_tensor(rstd_all[:], ve_all[:], half_neg_all[:], ALU.pow).then_inc(c_rstd, 1)
                pool.wait_ge(d_zf, 16)
                pool.wait_ge(d_slot, 2)
                pool.wait_ge(d_xn, TILES)
                for t in range(TILES):
                    for k in range(2):
                        pool.indirect_dma_start(out=sorted_x, out_offset=bass.IndirectOffsetOnAxis(ap=slot[k][:, t:t + 1], axis=0),
                                                in_=xn[:, t * D:(t + 1) * D], in_offset=None).then_inc(d_sc, 16)
                pool.wait_ge(d_sc, 2 * TILES * 16)

                def load(i, parity):
                    pool.wait_ge(e_xtr, i + 1)
                    pool.dma_start(x_in[parity][:], sorted_x[bass.ds(i * P, P), :]).then_inc(e_ld[parity], 16)

                def step(i, parity):
                    if not static(i) or i + 2 < MTILES:
                        load(i + 2, parity)
                    pool.wait_ge(e_y, i + 2)
                    pool.dma_start(sorted_y[bass.ds(i * P, P), :], y_out[parity][:]).then_inc(e_st[parity], 16)

                load(0, 0)
                load(1, 1)
                tile_loop(pool, step)
                pool.wait_ge(e_st[0], 16 * ((MTILES + 1) // 2))
                pool.wait_ge(e_st[1], 16 * (MTILES // 2))
                for t in range(TILES):
                    if t >= 8:
                        pool.wait_ge(d_out, 2 * (t - 8) + 2)
                    for k in range(2):
                        pool.indirect_dma_start(out=xn[:, (2 * t + k) % 16 * D:((2 * t + k) % 16 + 1) * D], out_offset=None,
                                                in_=sorted_y,
                                                in_offset=bass.IndirectOffsetOnAxis(ap=slot[k][:, t:t + 1], axis=0)).then_inc(d_got[t % 8], 16)

            def unit_parts(c, b, j):
                u = b * KVH + j
                f = q_f[j % 2][:].rearrange("p (t c) -> p t c", t=ST)
                fh = q_f[j % 2][:].rearrange("p (n c) -> p n c", c=HD)
                qs = q_s[j % 4][:].rearrange("p (n c) -> p n c", c=64)
                ks = k_s[j % 2][:].rearrange("p (t a c) -> p t a c", a=2, c=64)
                xs = tiles(X, b * ST, ST).rearrange("p (t c) -> p t c", c=D)[:, :, j * 64:(j + 1) * 64]
                mean = mv_all[:, bass.ds(b * 2 * ST, 2 * ST)].rearrange("p (t c) -> p t c", c=2)[:, :, 0:1]
                r = rstd_all[:, bass.ds(b * ST, ST)].rearrange("p (t c) -> p t c", c=1)
                cx = tiles(ctx_c, b * ST, ST, CTX).rearrange("p (t c) -> p t c", c=CTX)[:, :, j * HD:(j + 1) * HD]
                cx2 = cx.rearrange("p t (a c) -> p t a c", a=1).broadcast_to([P, ST, 2, HD])
                pool.wait_ge(c_tk, u + 1)
                pool.wait_ge(c_tqe, 2 * u + 2)
                pool.sem_inc(pool_waited, 1)
                c.step(nc.gpsimd.tensor_tensor(f, xs, mean.broadcast_to([P, ST, 64]), ALU.subtract))
                c.step(nc.gpsimd.tensor_tensor(f, f, r.broadcast_to([P, ST, 64]), ALU.mult))
                c.inc(nc.gpsimd.tensor_copy(qs[:, :, 0:HD], fh))
                c.inc(nc.gpsimd.tensor_copy(ks[:, :, :, 0:HD], cx2))
                c.step(nc.gpsimd.tensor_copy(v_u[j % 8][:].rearrange("p (t c) -> p t c", c=32)[:, :, 0:HD], cx))
                c.inc(nc.gpsimd.tensor_copy(qs[:, :, 2 * HD:3 * HD], fh))
                c.inc(nc.gpsimd.tensor_copy(ks[:, :, :, HD:2 * HD], cx2))
                nc.gpsimd.memset(qs[:, :, 48:50].bitcast(F32), 0.0).then_inc(c_prep, 1)
                nc.gpsimd.tensor_tensor(qs[:, :, HD:2 * HD], fh, qs[:, :, 0:HD], ALU.subtract).then_inc(c_prep, 1)
                nc.gpsimd.tensor_tensor(ks[:, :, :, 2 * HD:3 * HD], cx2, ks[:, :, :, 0:HD], ALU.subtract).then_inc(c_prep, 1)

            pool.wait_ge(pool_const, 3)
            pool.wait_ge(ld_const, 5 * 16)
            nc.gpsimd.tensor_copy(ident_b[:], ident[:]).then_inc(pool_const, 1)
            with pool.Fori(0, BATCH) as b:
                c.enter(b, ST)
                phase_a(b)
                c.leave(BATCH)
            with pool.Fori(0, BATCH) as b:
                inverse_root(2 * BATCH + b + 1)
                phase_b(b)
            phase_c(c)
            phase_d()

        @block.scalar
        def _(act):
            def context_t():
                for b in range(BATCH):
                    act.wait_ge(ctx_t_ps, b + 1)
                    nc.scalar.activation(ctx_t[:, b * SEQ:(b + 1) * SEQ], bank[b], ACT.Copy).then_inc(ctx_t_sb, 1)
                act.wait_ge(ctx_t_ps, BATCH + 1)
                nc.scalar.activation(wk_t[:], bank[4][:, 0:CTX], ACT.Copy).then_inc(ctx_t_sb, 1)

            def phase_a(b):
                act.wait_ge(a_kvt, b + 1)
                nc.scalar.activation(kv_t[:], bank[2], ACT.Identity, bias=bk_col[:, 0:1]).then_inc(a_kvt_sb, 1)
                for st in range(ST):
                    act.wait_ge(a_trans, b * ST + st + 1)
                    nc.scalar.activation(
                        a_pt[:].rearrange("p (k n) -> p k n", k=DC)[:, :, st * P:(st + 1) * P],
                        bank[st % 2].rearrange("p (k n) -> p k n", k=DC), ACT.Copy).then_inc(a_trans_sb, 1)
                act.wait_ge(a_kv, b + 1)
                nc.scalar.activation(kv[:], bank[3], ACT.Copy).then_inc(a_kv_sb, 1)
                act.wait_ge(a_out, b + 1)
                nc.scalar.activation(o_t[:], bank[2], ACT.Copy).then_inc(a_out_sb, 1)
                for st in range(ST):
                    act.wait_ge(a_neg, b * ST + st + 1)
                    nc.scalar.activation(a_e[:, st * SEQ:(st + 1) * SEQ], a_z[:, st * SEQ:(st + 1) * SEQ], ACT.Exp,
                                         bias=a_mx[:, st:st + 1], accum_out=a_sum[:, st:st + 1]).then_inc(a_exp, 1)

            def weight_abs(w):
                act.wait_ge(ld_raw[w], 16)
                if w:
                    act.wait_ge(w_abs, w)
                nc.scalar.activation(wd_t[:], raw[w % 2][:], ACT.Abs, accum_out=abs_sum[:, w:w + 1]).then_inc(w_abs, 1)

            def weights():
                for w in range(2):
                    wt = wgu_t[w][:].rearrange("p (k f) -> p k f", k=DC)
                    with act.Fori(0, FC // 2) as i:
                        for h in range(2):
                            act.wait_ge(w_tp, 2 + w * FC + 2 * i + h + 1)
                            nc.scalar.activation(wt[:, :, bass.ds((2 * i + h) * P, P)], t_view(4 + h), ACT.Copy).then_inc(w_evac, 1)
                    if w == 0:
                        weight_abs_down()
                wt = wd_t[:].rearrange("p (f h) -> p f h", f=FC)
                with act.Fori(0, DC) as hc:
                    for q in range(4):
                        act.wait_ge(w_tp, 2 + 2 * FC + 4 * hc + q + 1)
                        nc.scalar.activation(wt[:, 4 * q:4 * q + 4, bass.ds(hc * P, P)], t_view(4 + q % 2), ACT.Copy).then_inc(w_evac, 1)

            def weight_abs_down():
                act.wait_ge(ld_raw[2], 16)
                act.wait_ge(w_abs, 2)
                nc.scalar.activation(wd_t[:], raw[0][:], ACT.Abs, accum_out=abs_sum[:, 2:3]).then_inc(w_abs, 1)

            def t_view(n):
                return bank_b[n][:, 0:512].rearrange("p (k n) -> p k n", k=4)

            def phase_b(b):
                for st in range(ST):
                    act.wait_ge(b_trans, b * ST + st + 1)
                    nc.scalar.activation(h_hi[:, st * D:(st + 1) * D], bank[st % 2], ACT.Copy).then_inc(b_trans_sb, 1)
                act.wait_ge(b_fac, b + 1)
                for st in range(ST):
                    nc.scalar.activation(h_b[:, st * D:(st + 1) * D], bank[4 + st], ACT.Identity,
                                         bias=magic[:, 0:1], scale=fac[:, st:st + 1]).then_inc(b_tq, 1)
                act.wait_ge(b_sps, b + 1)
                nc.scalar.activation(scale_rows[:], bank[0], ACT.Copy).then_inc(b_sbc, 1)
                for a in range(2):
                    with act.Fori(0, 4) as i:
                        for h in range(2):
                            n = b * FC + a * 8 + 2 * i + h
                            act.wait_ge(b_g, 2 + n + 1)
                            act.wait_ge(b_y, n + 1)
                            nc.scalar.activation(g_silu[h][:], g_s[h][:], ACT.Silu, scale=w_mean[:, 0:1]).then_inc(b_sl, 1)

                def first_part(st):
                    act.wait_ge(b_rot, 2 * (b * ST + st) + 2)
                    nc.scalar.activation(token_tile(Z_hi, st), token_tile(Y, st), ACT.Copy).then_inc(b_zhi, 1)

                def transposed(n):
                    act.wait_ge(b_tr, 1 + n + 1)
                    nc.scalar.activation(q2_t[:], psum[:, 0:1024].bitcast(BF16), ACT.Copy).then_inc(b_q2ts, 1)

                first_part(0)
                first_part(1)
                act.wait_ge(b_y, 2 + (b + 1) * FC)
                for st in range(ST):
                    n = b * ST + st
                    if st >= 2:
                        act.wait_ge(b_tq2, 1 + n - 1)
                    for g in range(4):
                        act.wait_ge(b_z, 4 * n + g + 1)
                        nc.scalar.activation(z_s[st % 2][:, g * D:(g + 1) * D], bank[4 + g], ACT.Copy).then_inc(b_zc, 1)
                    if st > 0:
                        transposed(n - 1)
                    act.wait_ge(b_fac2, n + 1)
                    act.wait_ge(b_q2, n + 1)
                    nc.scalar.activation(h_b[:], z_s[st % 2][:], ACT.Identity, bias=magic[:, 0:1],
                                         scale=fac2[:, st:st + 1]).then_inc(b_tq2, 1)
                    if st + 2 < ST:
                        first_part(st + 2)
                transposed(b * ST + ST - 1)

            def attention(u, j, there):
                m, mj = u + 2, (j + 2) % 8

                def evac_parts(out, job, n, done):
                    act.wait_ge(job, n)
                    nc.scalar.activation(out[:], bank[7], ACT.Copy).then_inc(done, 1)

                for i in range(PAIRS):
                    if i in (1, 2) and there(m - 1):
                        p = i - 1
                        evac_parts(q_e[(mj + 1) % 2][p], c_tqe, 8 + 2 * (m - 1) + p + 1, c_eqe)
                    if i == 3 and there(m + 1):
                        r = (mj + 1) % 4
                        act.wait_ge(c_tk, 2 + m + 2)
                        nc.scalar.activation(k_lo[r][0:64, :], bank[7][0:64, :], ACT.Copy).then_inc(c_ek, 1)
                        nc.scalar.activation(k_hi[r][64:P, :], bank[7][64:P, :], ACT.Copy).then_inc(c_ek, 1)
                    if i == 4 and there(m + 1):
                        evac_parts(q_m[0], c_tqm, 2 * (m + 1) + 1, c_eqm)
                    if there(u):
                        n = PAIRS * u + i
                        act.wait_ge(c_s, n + 1)
                        act.wait_ge(c_pv, n + 1)
                        nc.scalar.activation(prob[i % 2][:], psum[:, (2 + 2 * (i % 2)) * 512:(4 + 2 * (i % 2)) * 512], ACT.Exp,
                                             scale=HD ** -0.5).then_inc(c_e, 1)
                if there(m + 1):
                    if there(m):
                        act.wait_ge(c_mx, 16 * (m + 1))
                    evac_parts(q_m[1], c_tqm, 2 * (m + 1) + 2, c_eqm)

            def phase_d():
                for t in range(TILES):
                    act.wait_ge(d_tr, t + 1)
                    nc.scalar.activation(xn_t[t % 2][:], bank[2 + t % 2], ACT.Copy).then_inc(d_trs, 1)
                act.wait_ge(d_gap, 1)
                nc.scalar.activation(gap_e[:], gap[:], ACT.Exp).then_inc(d_gap_e, 1)

                def step(i, parity):
                    for half in range(2):
                        act.wait_ge(e_gu, 2 * i + half + 1)
                        act.wait_ge(e_h, 2 * i + half + 1)
                        nc.scalar.activation(g_silu_d[half][:], bank[2 * half], ACT.Silu).then_inc(e_silu, 1)
                    act.wait_ge(e_htr, 2 * i + 1)
                    nc.scalar.activation(h_dt[:, 0:512], bank[5], ACT.Copy).then_inc(e_ht0, 1)

                tile_loop(act, step)

            def phase_c():
                act.wait_ge(c_const, 33)
                act.wait_ge(c_tk, 2 + 1)
                nc.scalar.activation(k_lo[0][0:64, :], bank[7][0:64, :], ACT.Copy).then_inc(c_ek, 1)
                nc.scalar.activation(k_hi[0][64:P, :], bank[7][64:P, :], ACT.Copy).then_inc(c_ek, 1)
                for p in range(2):
                    act.wait_ge(c_tqm, p + 1)
                    nc.scalar.activation(q_m[p][:], bank[7], ACT.Copy).then_inc(c_eqm, 1)
                slots(act, attention)

            act.sem_inc(w_evac, 2)
            act.sem_inc(b_tq2, 1)
            act.wait_ge(ld_const, 5 * 16)
            act.wait_ge(pool_const, 4)
            context_t()
            weight_abs(0)
            weight_abs(1)
            with act.Fori(0, BATCH) as b:
                phase_a(b)
            weights()
            nc.scalar.activation(silu_first[:], magic[:], ACT.Silu).then_inc(act_step, 1)
            act.wait_ge(ld_had, 16)
            nc.scalar.activation(had[:], h_b[:], ACT.Copy).then_inc(had_ready, 1)
            with act.Fori(0, BATCH) as b:
                phase_b(b)
            act.sem_inc(c_e, 2)
            phase_c()
            phase_d()

        @block.vector
        def _(dve):
            c = Count(dve, dve_step)

            def layer_norm(b, out_tiles, group, written):
                for st in range(ST):
                    c.inc(nc.vector.bn_stats(st6[:, 6 * st:6 * st + 6], tiles(X, b * ST + st)))
                c.wait()
                c.inc(nc.vector.memset(var_eps[:, 0:1], 1.0))
                for st in range(ST):
                    c.inc(nc.vector.bn_aggr(mv[:, 2 * st:2 * st + 2], st6[:, 6 * st:6 * st + 6]))
                c.wait()
                nc.vector.tensor_scalar(var_eps[:], mv[:, 1:2 * ST:2], 1.0, EPS_LN, ALU.mult, ALU.add).then_inc(ln_var, 1)
                dve.wait_ge(ln_rstd, group)
                for st in range(ST):
                    nc.vector.tensor_scalar(out_tiles[:, st * D:(st + 1) * D], tiles(X, b * ST + st),
                                            mv[:, 2 * st:2 * st + 1], rstd[:, st:st + 1],
                                            ALU.subtract, ALU.mult).then_inc(written, 1)

            def phase_a(b):
                layer_norm(b, a_p, 2 * b + 1, a_normed)
                dve.wait_ge(a_sim, b * ST + ST)
                for st in range(ST):
                    c.inc(nc.vector.bn_stats(st6[:, 6 * st:6 * st + 6], bank[4 + st]))
                c.wait()
                c.inc(nc.vector.memset(var_eps[:, 0:1], 1.0))
                for st in range(ST):
                    c.inc(nc.vector.bn_aggr(mv[:, 2 * st:2 * st + 2], st6[:, 6 * st:6 * st + 6]))
                c.wait()
                nc.vector.tensor_scalar(var_eps[:], mv[:, 1:2 * ST:2], SCORE_SCALE ** 2, EPS_SCORE,
                                        ALU.mult, ALU.add).then_inc(ln_var, 1)
                dve.wait_ge(ln_rstd, 2 * b + 2)
                c.step(nc.vector.tensor_scalar(a_rs[:], rstd[:], SCORE_SCALE, None, ALU.mult))
                for st in range(ST):
                    nc.vector.tensor_scalar(a_z[:, st * SEQ:(st + 1) * SEQ], bank[4 + st],
                                            mv[:, 2 * st:2 * st + 1], a_rs[:, st:st + 1],
                                            ALU.subtract, ALU.mult).then_inc(a_simz, 1)
                for st in range(ST):
                    dve.wait_ge(a_zg, b * ST + st + 1)
                    nc.vector.tensor_reduce(a_mx[:, st:st + 1], a_z[:, st * SEQ:(st + 1) * SEQ], AX.X, ALU.max,
                                            negate=True).then_inc(a_neg, 1)
                dve.wait_ge(a_exp, b * ST + ST)
                c.step(nc.vector.reciprocal(a_rs[:], a_sum[:]))
                for st in range(ST):
                    xt = tiles(X, b * ST + st)
                    nc.vector.scalar_tensor_tensor(out=xt, in0=a_e[:, st * SEQ:(st + 1) * SEQ], scalar=a_rs[:, st:st + 1],
                                                   in1=xt, op0=ALU.mult, op1=ALU.add).then_inc(a_done, 1)

            def weight_scale(w):
                dve.wait_ge(w_tot, w + 1)
                c.step(nc.vector.tensor_scalar(w_mean[:, w:w + 1], bank[3][:, w:w + 1], 1.0 / (FF * D), EPS_Q, ALU.mult, ALU.max))
                c.inc(nc.vector.tensor_scalar(w_thr[:, w:w + 1], w_mean[:, w:w + 1], 0.5, None, ALU.mult))
                c.step(nc.vector.tensor_scalar(w_nthr[:, w:w + 1], w_mean[:, w:w + 1], -0.5, None, ALU.mult))

            def ternary(w, unit, src, h):
                dve.wait_ge(w_tp, unit + 1)
                c.step(nc.vector.tensor_scalar(neg[h][:], src, w_nthr[:, w:w + 1], None, ALU.is_lt))
                nc.vector.scalar_tensor_tensor(out=tern[h][:], in0=src, scalar=w_thr[:, w:w + 1], in1=neg[h][:],
                                               op0=ALU.is_gt, op1=ALU.subtract).then_inc(w_tern, 1)

            def weights():
                for w in range(3):
                    weight_scale(w)
                    with dve.Fori(0, FC // 2) as i:
                        c.enter(i, 2)
                        for h in range(2):
                            ternary(w, w * FC + 2 * i + h, raw[w % 2][:, bass.ds((2 * i + h) * 512, 512)], h)
                        c.leave(FC // 2)

            def phase_b(b):
                layer_norm(b, h_b, 2 * BATCH + b + 1, b_normed)
                for st in range(ST):
                    dve.wait_ge(b_trans_sb, b * ST + st + 1)
                    nc.vector.tensor_tensor(h_lo[:, st * D:(st + 1) * D], bank[st % 2], h_hi[:, st * D:(st + 1) * D],
                                            ALU.subtract).then_inc(b_lo, 1)
                for st in range(ST):
                    dve.wait_ge(b_fw, b * ST + st + 1)
                    c.inc(nc.vector.tensor_reduce(am[:, st:st + 1], bank[4 + st], AX.X, ALU.max, apply_absolute_value=True))
                c.wait()
                c.step(nc.vector.tensor_scalar(am_c[:], am[:], HAD_D, EPS_Q, ALU.mult, ALU.max))
                c.inc(nc.vector.tensor_scalar(tok_scale[:], am_c[:], 1.0 / 127.0, None, ALU.mult))
                c.step(nc.vector.reciprocal(am_r[:], am_c[:]))
                nc.vector.tensor_scalar(fac[:], am_r[:], 127.0 * HAD_D, None, ALU.mult).then_inc(b_fac, 1)
                for st in range(ST):
                    last = nc.vector.tensor_scalar(diag[:, st * P:(st + 1) * P], ident[:], tok_scale[:, st:st + 1], None, ALU.mult)
                last.then_inc(b_dg, 1)
                c.step(nc.vector.tensor_scalar(inner_scale[:], tok_scale[:], w_mean[:, 1:2], HAD_FF, ALU.mult, ALU.mult))
                for st in range(ST):
                    dve.wait_ge(b_tq, b * ST + st + 1)
                    nc.vector.tensor_scalar(q_b[:, st * D:(st + 1) * D], h_b[:, st * D:(st + 1) * D], MAGIC, 127.0,
                                            ALU.subtract, ALU.min).then_inc(b_q, 1)
                for st in range(ST):
                    dve.wait_ge(b_qt, b * ST + st + 1)
                    nc.vector.tensor_copy(q_t[:].rearrange("p (k n) -> p k n", k=DC)[:, :, st * P:(st + 1) * P],
                                          bank_b[2 + st % 2][:, 0:512].rearrange("p (k n) -> p k n", k=DC)).then_inc(b_qts, 1)
                for a in range(2):
                    with dve.Fori(0, 4) as i:
                        n = b * FC + a * 8 + 2 * i
                        dve.wait_ge(b_sbc, b + 1)
                        for h in range(2):
                            dve.wait_ge(b_gp, n + h + 1)
                            nc.vector.tensor_tensor(g_s[h][:], bank[h], scale_rows[:], ALU.mult).then_inc(b_g, 1)
                        for h in range(2):
                            dve.wait_ge(b_sl, n + h + 1)
                            dve.wait_ge(b_up, n + h + 1)
                            nc.vector.tensor_tensor(Y[:, bass.ds((8 * a + i + 4 * h) * SEQ, SEQ)], bank[2 + h], g_silu[h][:],
                                                    ALU.mult).then_inc(b_y, 1)

                def second_stage(st):
                    x0, x1 = token_tile(Z, st)[:, 0:8], token_tile(Z, st)[:, 8:16]
                    nc.vector.tensor_tensor(token_tile(Y, st)[:, 0:8], x0, x1, ALU.add).then_inc(b_rot, 1)
                    nc.vector.tensor_tensor(token_tile(Y, st)[:, 8:16], x0, x1, ALU.subtract).then_inc(b_rot, 1)

                dve.wait_ge(b_half, (b + 1) * FC)
                second_stage(0)
                dve.wait_ge(b_zhi, b * ST + 1)
                nc.vector.tensor_tensor(token_tile(Y_lo, 0), token_tile(Y, 0), token_tile(Z_hi, 0),
                                        ALU.subtract).then_inc(b_zlo0, 1)
                second_stage(1)
                for st in range(ST + 1):
                    n = b * ST + st
                    if st < ST:
                        s = slice(st, st + 1)
                        dve.wait_ge(b_zc, 4 + 4 * (n + 1))
                        c.step(nc.vector.tensor_reduce(am2[:, s], z_s[st % 2][:], AX.X, ALU.max, apply_absolute_value=True))
                        c.step(nc.vector.tensor_scalar(am2_c[:, s], am2[:, s], inner_scale[:, s], EPS_Q, ALU.mult, ALU.max))
                        c.inc(nc.vector.tensor_scalar(deq[:, s], am2_c[:, s], w_mean[:, 2:3], 1.0 / 127.0, ALU.mult, ALU.mult))
                        c.step(nc.vector.reciprocal(am2_r[:, s], am2_c[:, s]))
                        nc.vector.tensor_scalar(fac2[:, s], am2_r[:, s], inner_scale[:, s], 127.0, ALU.mult, ALU.mult).then_inc(b_fac2, 1)
                        if st + 2 < ST:
                            second_stage(st + 2)
                        dve.wait_ge(b_tq2, 1 + n + 1)
                        dve.wait_ge(b_tr, n + 1)
                        nc.vector.tensor_scalar(q_b[:], h_b[:], MAGIC, 127.0, ALU.subtract, ALU.min).then_inc(b_q2, 1)
                    if st > 0:
                        dve.wait_ge(b_dn, n)
                        xt = tiles(X, n - 1)
                        nc.vector.scalar_tensor_tensor(out=xt, in0=bank[2 + (st - 1) % 2], scalar=deq[:, st - 1:st], in1=xt,
                                                       op0=ALU.mult, op1=ALU.add).then_inc(b_x, 1)

            def attention(u, j, there):
                m, mj = u + 2, (j + 2) % 8
                for i in range(PAIRS):
                    if i == 1 and there(u - 1):
                        dve.wait_ge(c_pv, 2 + PAIRS * u)
                        nc.vector.tensor_copy(att_t[:], bank[6]).then_inc(c_oe, 1)
                    if i == 6 and there(u - 1):
                        add_attended(u - 1, (j - 1) % 8)
                    if there(m):
                        for g in (2 * i, 2 * i + 1):
                            h, st = g // ST, g % ST
                            dve.wait_ge(c_mx, 16 * m + g + 1)
                            nc.vector.tensor_reduce(neg_max[mj % 2][:, st * GROUP + h:st * GROUP + h + 1], bank[g % 2],
                                                    AX.X, ALU.max, negate=True).then_inc(c_red, 1)
                if there(m):
                    qs = q_s[mj % 4][:].rearrange("p (n c) -> p n c", c=64)
                    nm = neg_max[mj % 2][:].rearrange("p (n c) -> p n c", c=1)
                    dve.wait_ge(c_red, 2 + 16 * (m + 1))
                    dve.wait_ge(c_prep, 3 * (m + 1))
                    c.step(nc.vector.tensor_copy(qs[:, :, 48:49], nm))
                    nc.vector.tensor_tensor(qs[:, :, 49:50], nm, qs[:, :, 48:49], ALU.subtract).then_inc(c_m, 1)

            def phase_d():
                for t in range(TILES):
                    c.inc(nc.vector.bn_stats(st6_all[:, 6 * t:6 * t + 6], X[:, t * D:(t + 1) * D]))
                c.wait()
                for t in range(TILES):
                    c.inc(nc.vector.bn_aggr(mv_all[:, 2 * t:2 * t + 2], st6_all[:, 6 * t:6 * t + 6]))
                c.wait()
                nc.vector.tensor_scalar(ve_all[:], mv_all[:, 1:2 * TILES:2], 1.0, EPS_LN, ALU.mult, ALU.add).then_inc(c_var, 1)
                dve.wait_ge(c_rstd, 2)
                for t in range(TILES):
                    nc.vector.tensor_scalar(xn[:, t * D:(t + 1) * D], X[:, t * D:(t + 1) * D], mv_all[:, 2 * t:2 * t + 1],
                                            rstd_all[:, t:t + 1], ALU.subtract, ALU.mult).then_inc(d_xn, 1)
                dve.wait_ge(d_lg, TILES)
                c.step(nc.vector.tensor_copy(lg[:], bank[0][:, 0:TILES * EXPERTS]))
                for t in range(TILES):
                    s = slice(t * EXPERTS, (t + 1) * EXPERTS)
                    c.inc(nc.vector.max(top[:, s], lg[:, s]))
                c.wait()

                def by_tile(a, e=EXPERTS):
                    return a.rearrange("p (t e) -> p t e", e=e)

                dve.wait_ge(ld_d, 4 * 16)
                top3 = by_tile(top[:])
                nc.vector.tensor_tensor(by_tile(gap[:], 1), top3[:, :, 1:2], top3[:, :, 0:1], ALU.subtract).then_inc(d_gap, 1)
                for k in range(2):
                    largest = top3[:, :, k:k + 1].broadcast_to([P, TILES, EXPERTS])
                    c.step(nc.vector.tensor_tensor(by_tile(picked[k][:]), by_tile(lg[:]), largest, ALU.is_equal))
                    c.step(nc.vector.tensor_tensor(picked[k][:], picked[k][:], num_e[:], ALU.mult))
                    if k == 1:
                        c.step(nc.vector.tensor_tensor(both[:], picked[1][:], chosen[0][:], ALU.mult))
                        c.step(nc.vector.tensor_tensor(picked[1][:], picked[1][:], both[:], ALU.subtract))
                    c.step(nc.vector.tensor_reduce(by_tile(slot_f[k][:], 1), by_tile(picked[k][:]), AX.X, ALU.max))
                    number = by_tile(slot_f[k][:], 1).broadcast_to([P, TILES, EXPERTS])
                    c.step(nc.vector.tensor_tensor(by_tile(chosen[k][:]), by_tile(num_e[:]), number, ALU.is_equal))
                nc.vector.tensor_tensor(both[:], chosen[0][:], chosen[1][:], ALU.add).then_inc(d_both, 1)
                c.inc(nc.vector.memset(running[:, 0:EXPERTS], 0.0))
                n = TILES * EXPERTS
                dve.wait_ge(d_rank, 1)
                for t in range(TILES):
                    c.wait()
                    s = slice(t * EXPERTS, (t + 1) * EXPERTS)
                    c.inc(nc.vector.tensor_tensor(running[:, (t + 1) * EXPERTS:(t + 2) * EXPERTS], running[:, s],
                                                  bank[1][:, n + t * EXPERTS:n + (t + 1) * EXPERTS], ALU.add))
                c.wait()
                c.step(nc.vector.tensor_tensor(slot_e[:], running[:, 0:n], bank[1][:, 0:n], ALU.add))
                count = running[:, n:n + EXPERTS]
                c.step(nc.vector.tensor_scalar(row8_i["count"][:], count, float(P - 1), None, ALU.add))
                c.step(nc.vector.tensor_scalar(row8_i["tiles"][:], row8_i["count"][:], 7, None, ALU.logical_shift_right))
                c.step(nc.vector.tensor_copy(row8["tiles"][:], row8_i["tiles"][:]))
                c.step(nc.vector.tensor_copy(row8["end"][:, 0:1], row8["tiles"][:, 0:1]))
                for e in range(1, EXPERTS):
                    c.step(nc.vector.tensor_tensor(row8["end"][:, e:e + 1], row8["end"][:, e - 1:e], row8["tiles"][:, e:e + 1], ALU.add))
                c.step(nc.vector.tensor_tensor(row8["first"][:], row8["end"][:], row8["tiles"][:], ALU.subtract))
                c.step(nc.vector.tensor_scalar(row8["first"][:], row8["first"][:], float(P), None, ALU.mult))
                c.step(nc.vector.tensor_tensor(by_tile(slot_e[:]), by_tile(slot_e[:]),
                                               row8["first"][:].rearrange("p (t e) -> p t e", t=1).broadcast_to([P, TILES, EXPERTS]), ALU.add))
                for k in range(2):
                    c.step(nc.vector.tensor_tensor(picked[k][:], slot_e[:], chosen[k][:], ALU.mult))
                    c.step(nc.vector.tensor_reduce(by_tile(slot_f[k][:], 1), by_tile(picked[k][:]), AX.X, ALU.add))
                    nc.vector.tensor_copy(slot[k][:], slot_f[k][:]).then_inc(d_slot, 1)
                plan_tiles()
                dve.wait_ge(d_gap_e, 1)
                c.step(nc.vector.tensor_scalar(gap_1[:], gap_e[:], 1.0, None, ALU.add))
                c.step(nc.vector.reciprocal(top_w[0][:], gap_1[:]))
                c.step(nc.vector.tensor_tensor(top_w[1][:], gap_e[:], top_w[0][:], ALU.mult))

                def step(i, parity):
                    if static(i) and i == 0:
                        move_x(0, 0)
                    for half in range(2):
                        dve.wait_ge(e_silu, 2 * i + half + 1)
                        dve.wait_ge(e_gu, 2 * i + half + 1)
                        nc.vector.tensor_tensor(h_d[:, half * 512:(half + 1) * 512], bank[2 * half + 1], g_silu_d[half][:],
                                                ALU.mult).then_inc(e_h, 1)
                    if not static(i) or i > 0:
                        move_y(i - 1, 1 - parity)
                    if not static(i) or i + 1 < MTILES:
                        move_x(i + 1, 1 - parity)
                    dve.wait_ge(e_htr, 2 * i + 2)
                    nc.vector.tensor_copy(h_dt[:, 512:1024], bank[6]).then_inc(e_ht1, 1)

                def move_x(i, parity):
                    dve.wait_ge(e_xtr, 2 + i + 1)
                    nc.vector.tensor_copy(x_t[parity][:], bank[4]).then_inc(e_xt, 1)

                def move_y(i, parity):
                    dve.wait_ge(e_wo, i + 2)
                    if not (static(i) and i < 2):
                        dve.wait_ge(e_st[parity], 8 * (i - parity))
                    nc.vector.tensor_copy(y_out[parity][:], bank[7]).then_inc(e_y, 1)

                tile_loop(dve, step)
                move_y(MTILES - 1, 0)
                for t in range(TILES):
                    xt = X[:, t * D:(t + 1) * D]
                    dve.wait_ge(d_got[t % 8], 32 * (t // 8 + 1))
                    for k in range(2):
                        nc.vector.scalar_tensor_tensor(out=xt, in0=xn[:, (2 * t + k) % 16 * D:((2 * t + k) % 16 + 1) * D],
                                                       scalar=top_w[k][:, t:t + 1], in1=xt, op0=ALU.mult,
                                                       op1=ALU.add).then_inc(d_out, 1)
                        dve.wait_ge(d_out, 2 * t + k + 1)

            def plan_tiles():
                def by_mt(a, e=EXPERTS):
                    return a.rearrange("p (t e) -> p t e", e=e)

                def over_tiles(a):
                    return a.rearrange("p (t e) -> p t e", t=1).broadcast_to([1, MTILES, EXPERTS])

                c.inc(nc.vector.tensor_scalar(row8_i["wait"][0:1, :], row8["end"][0:1, :], 1.0, None, ALU.add))
                num = by_mt(num_tile[:])
                c.step(nc.vector.tensor_tensor(by_mt(past_end[:]), num, over_tiles(row8["end"][0:1, :]), ALU.is_ge))
                c.step(nc.vector.tensor_reduce(by_mt(mt["expert"][:], 1), by_mt(past_end[:]), AX.X, ALU.add))
                plan3 = plan[:].rearrange("p (t c) -> p t c", c=3)
                c.step(nc.vector.tensor_scalar(mt["expert"][:], mt["expert"][:], float(EXPERTS - 1), None, ALU.min))
                c.inc(nc.vector.tensor_copy(mt_i["expert"][:], mt["expert"][:]))
                c.inc(nc.vector.tensor_scalar(mt_i["next"][:], mt["expert"][:], 1.0, None, ALU.add))
                c.step(nc.vector.tensor_scalar(mt["first"][:], mt["expert"][:], 0.0, None, ALU.is_equal))
                c.inc(nc.vector.tensor_scalar(mt_i["half"][:], mt_i["expert"][:], 1, None, ALU.logical_shift_right))
                c.step(nc.vector.tensor_scalar(mt_i["half_up"][:], mt_i["next"][:], 1, None, ALU.logical_shift_right))
                c.inc(nc.vector.tensor_copy(mt["half"][:], mt_i["half"][:]))
                c.step(nc.vector.tensor_copy(mt["half_up"][:], mt_i["half_up"][:]))
                c.step(nc.vector.scalar_tensor_tensor(out=mt["parity"][:], in0=mt["half"][:], scalar=-2.0, in1=mt["expert"][:],
                                                      op0=ALU.mult, op1=ALU.add))
                c.step(nc.vector.tensor_tensor(mt["half_up"][:], mt["half_up"][:], mt["first"][:], ALU.add))
                c.inc(nc.vector.tensor_scalar(plan3[:, :, 0:1], by_mt(mt["parity"][:], 1), float(EXPERT_COLS), None, ALU.mult))
                c.inc(nc.vector.tensor_scalar(plan3[:, :, 1:2], by_mt(mt["half"][:], 1), 48.0, 48.0, ALU.mult, ALU.add))
                c.step(nc.vector.tensor_scalar(plan3[:, :, 2:3], by_mt(mt["half_up"][:], 1), 48.0, None, ALU.mult))
                nc.vector.memset(last_free[:], 0.0).then_inc(d_plan, 1)

            def add_attended(v, vj):
                dve.wait_ge(c_to, v + 1)
                o = bank[7].rearrange("p (n c) -> p n c", c=32)
                c.step(nc.vector.reciprocal(att_r[:].rearrange("p (n c) -> p n c", c=1), o[:, :, HD:HD + 1]))
                nc.vector.tensor_tensor(att_n[:].rearrange("p (n c) -> p n c", c=HD), o[:, :, 0:HD],
                                        att_r[:].rearrange("p (n c) -> p n c", c=1).broadcast_to([P, ST * GROUP, HD]),
                                        ALU.mult).then_inc(c_eo, 1)
                dve.wait_ge(c_eo, v + 1)
                xs = x_unit(v, vj)
                nc.vector.tensor_tensor(xs, xs, att_n[:].rearrange("p (t c) -> p t c", t=ST), ALU.add).then_inc(c_x, 1)
                dve.wait_ge(c_x, v + 1)

            def x_unit(v, vj):
                at = (v - vj) * (ST * D // KVH)
                return X[:, bass.ds(at, ST * D)].rearrange("p (t c) -> p t c", c=D)[:, :, vj * 64:(vj + 1) * 64]

            def phase_c():
                dve.wait_ge(b_x, BATCH * ST)
                for t in range(TILES):
                    c.inc(nc.vector.bn_stats(st6_all[:, 6 * t:6 * t + 6], X[:, t * D:(t + 1) * D]))
                c.wait()
                for t in range(TILES):
                    c.inc(nc.vector.bn_aggr(mv_all[:, 2 * t:2 * t + 2], st6_all[:, 6 * t:6 * t + 6]))
                c.wait()
                nc.vector.tensor_scalar(ve_all[:], mv_all[:, 1:2 * TILES:2], 1.0, EPS_LN, ALU.mult, ALU.add).then_inc(c_var, 1)
                slots(dve, attention, c, 2 * KVH)
            dve.sem_inc(b_g, 2)
            dve.sem_inc(b_y, 2)
            dve.sem_inc(b_q2, 1)
            dve.wait_ge(ld_x, 16)
            dve.wait_ge(pool_const, 3)
            with dve.Fori(0, BATCH) as b:
                c.enter(b, 2 * (2 * ST + 1) + 2)
                phase_a(b)
                c.leave(BATCH)
            dve.wait_ge(ld_const, 5 * 16)
            weights()
            dve.wait_ge(had_ready, 1)
            with dve.Fori(0, BATCH) as b:
                c.enter(b, 2 * ST + 1 + ST + 4 + 4 * ST)
                phase_b(b)
                c.leave(BATCH)
            dve.sem_inc(c_red, 2)
            dve.sem_inc(c_oe, 1)
            phase_c()
            dve.sem_inc(e_h, 2)
            dve.sem_inc(e_y, 1)
            phase_d()

        @block.tensor
        def _(pe):
            def context_t():
                pe.wait_ge(ld_ctx, 16)
                for b in range(BATCH):
                    for t in range(ST):
                        last = nc.tensor.transpose(bank[b][:, t * P:(t + 1) * P],
                                                   ctx_raw[:, (b * ST + t) * CTX:(b * ST + t + 1) * CTX], ident[:])
                    last.then_inc(ctx_t_ps, 1)
                nc.tensor.transpose(bank[4][:, 0:CTX], wk_sb[:], ident[:]).then_inc(ctx_t_ps, 1)

            def phase_a(b):
                nc.tensor.matmul(bank[2], wk_t[:], ctx_t[:, bass.ds(b * SEQ, SEQ)], start=True, stop=True).then_inc(a_kvt, 1)
                for st in range(ST):
                    pe.wait_ge(a_normed, b * ST + st + 1)
                    if st >= 2:
                        pe.wait_ge(a_trans_sb, b * ST + st - 1)
                    for k in range(DC):
                        last = nc.tensor.transpose(bank[st % 2][:, k * P:(k + 1) * P],
                                                   a_p[:, st * D + k * P:st * D + (k + 1) * P], ident[:])
                    last.then_inc(a_trans, 1)
                pe.wait_ge(a_kvt_sb, b + 1)
                for t in range(ST):
                    last = nc.tensor.transpose(bank[3][:, t * CTX:(t + 1) * CTX], kv_t[:, t * P:(t + 1) * P], ident[:])
                last.then_inc(a_kv, 1)
                pe.wait_ge(a_kv_sb, b + 1)
                pe.wait_ge(a_trans_sb, b * ST + ST)
                for k in range(DC):
                    last = nc.tensor.matmul(bank[2], kv[:, k * CTX:(k + 1) * CTX], a_pt[:, k * SEQ:(k + 1) * SEQ],
                                            start=(k == 0), stop=(k == DC - 1))
                last.then_inc(a_out, 1)
                pe.wait_ge(a_out_sb, b + 1)
                for st in range(ST):
                    nc.tensor.matmul(bank[4 + st], o_t[:, st * P:(st + 1) * P], kv_t[:], start=True,
                                     stop=True).then_inc(a_sim, 1)

            def weights():
                for w in range(3):
                    pe.wait_ge(w_abs, w + 1)
                    nc.tensor.matmul(bank[3][:, w:w + 1], ones[:], abs_sum[:, w:w + 1], start=True, stop=True).then_inc(w_tot, 1)
                    with pe.Fori(0, FC // 2) as i:
                        for h in range(2):
                            unit = w * FC + 2 * i + h
                            pe.wait_ge(w_tern, unit + 1)
                            pe.wait_ge(w_evac, unit + 1)
                            for j in range(4):
                                last = nc.tensor.transpose(bank_b[4 + h][:, j * P:(j + 1) * P], tern[h][:, j * P:(j + 1) * P], ident_b[:])
                            last.then_inc(w_tp, 1)

            def phase_b(b):
                def rotate(st):
                    pe.wait_ge(b_lo, b * ST + st + 1)
                    for k in range(DC):
                        for part, h in enumerate((h_hi, h_lo)):
                            last = nc.tensor.matmul(bank[4 + st], h[:, st * D + k * P:st * D + (k + 1) * P], had[:, k * D:(k + 1) * D],
                                                    start=(k + part == 0), stop=(k + part == DC))
                    last.then_inc(b_fw, 1)

                for st in range(ST):
                    pe.wait_ge(b_normed, b * ST + st + 1)
                    if st >= 2:
                        pe.wait_ge(b_lo, b * ST + st - 1)
                    for k in range(DC):
                        last = nc.tensor.transpose(bank[st % 2][:, k * P:(k + 1) * P],
                                                   h_b[:, st * D + k * P:st * D + (k + 1) * P], ident[:])
                    last.then_inc(b_trans, 1)
                    if st > 0:
                        rotate(st - 1)
                rotate(ST - 1)
                pe.wait_ge(b_dg, b + 1)
                for st in range(ST):
                    last = nc.tensor.matmul(bank[0][:, st * P:(st + 1) * P], ones[:], diag[:, st * P:(st + 1) * P], start=True, stop=True)
                last.then_inc(b_sps, 1)
                for st in range(ST):
                    pe.wait_ge(b_q, b * ST + st + 1)
                    if st >= 2:
                        pe.wait_ge(b_qts, b * ST + st - 1)
                    for k in range(DC):
                        last = nc.tensor.transpose(bank_b[2 + st % 2][:, k * P:(k + 1) * P],
                                                   q_b[:, st * D + k * P:st * D + (k + 1) * P], ident_b[:])
                    last.then_inc(b_qt, 1)
                for a in range(2):
                    with pe.Fori(0, 4) as i:
                        n = b * FC + a * 8 + 2 * i
                        pe.wait_ge(b_qts, b * ST + ST)
                        pe.wait_ge(b_sbc, b + 1)
                        for w, (freed, ready) in enumerate(((b_g, b_gp), (b_y, b_up))):
                            for h in range(2):
                                pe.wait_ge(freed, n + h + 1)
                                for k in range(DC):
                                    last = nc.tensor.matmul(bank[2 * w + h], wgu_t[w][:, bass.ds(k * FF + (8 * a + i + 4 * h) * P, P)],
                                                            q_t[:, k * SEQ:(k + 1) * SEQ], start=(k == 0), stop=(k == DC - 1))
                                last.then_inc(ready, 1)
                pe.wait_ge(b_y, 2 + (b + 1) * FC)
                for st in range(ST + 1):
                    n = b * ST + st
                    if st < ST:
                        if st == 0:
                            pe.wait_ge(b_zlo0, b + 1)
                        else:
                            pe.wait_ge(b_zlo, (ST - 1) * b + st)
                        for g in range(4):
                            pe.wait_ge(b_zc, 4 * n + g + 1)
                            for k in range(DC):
                                at = (g * DC + k) * SEQ + st * P
                                for part, y in enumerate((Z_hi, Y_lo)):
                                    last = nc.tensor.matmul(bank[4 + g], y[:, at:at + P], had[:, k * D:(k + 1) * D],
                                                            start=(k + part == 0), stop=(k + part == DC))
                            last.then_inc(b_z, 1)
                    if st > 0:
                        pe.wait_ge(b_q2, 1 + n)
                        for j in range(FC):
                            last = nc.tensor.transpose(bank_b[j // 8][:, (j % 8) * P:(j % 8 + 1) * P],
                                                       q_b[:, j * P:(j + 1) * P], ident_b[:])
                        last.then_inc(b_tr, 1)
                        pe.wait_ge(b_q2ts, n)
                        if st > 2:
                            pe.wait_ge(b_x, n - 2)
                        for j in range(FC):
                            last = nc.tensor.matmul(bank[2 + (st - 1) % 2], q2_t[:, j * P:(j + 1) * P], wd_t[:, j * D:(j + 1) * D],
                                                    start=(j == 0), stop=(j == FC - 1))
                        last.then_inc(b_dn, 1)

            free = []

            def bank_job(ready, inputs, done, freed):
                for s_, v_ in ready + free:
                    pe.wait_ge(s_, v_)
                for t, a in enumerate(inputs):
                    last = nc.tensor.transpose(bank[7][:, t * P:(t + 1) * P], a, ident[:])
                last.then_inc(done, 1)
                free[:] = [freed]

            def query_inputs(mj, p):
                q = q_s[mj % 4][:].bitcast(F32)
                return [q[:, (t * GROUP + 2 * p) * 64:(t * GROUP + 2 * p + 2) * 64] for t in range(ST)]

            def key_job(v, vj):
                k = k_s[vj % 2][:].bitcast(F32)
                bank_job([(c_prep, 3 * (v + 1))], [k[:, t * P:(t + 1) * P] for t in range(ST)], c_tk, (c_ek, 2 * (v + 1)))

            def attention(u, j, there):
                m, mj = u + 2, (j + 2) % 8

                def attend(n, i, vj):
                    t, p = i // 2, i % 2
                    pe.wait_ge(c_e, 2 + n + 1)
                    for h in range(2):
                        last = nc.tensor.matmul(bank[6][(2 * p + h) * 32:(2 * p + h + 1) * 32, :], v_u[vj % 8][:, t * 32:(t + 1) * 32],
                                                prob[i % 2][:, h * SEQ:(h + 1) * SEQ], start=(t == 0), stop=(t == ST - 1))
                    last.then_inc(c_pv, 1)

                if there(m):
                    free[:] = [(c_eqm, 2 * m + 2)]
                for i in range(PAIRS):
                    if i in (1, 2) and there(m - 1):
                        v, p = m - 1, i - 1
                        bank_job([(c_m, v + 1)], query_inputs(mj - 1, p), c_tqe, (c_eqe, 2 * v + p + 1))
                    if i == 3 and there(m + 1):
                        key_job(m + 1, mj + 1)
                    if i == 4 and there(m + 1):
                        bank_job([], query_inputs(mj + 1, 0), c_tqm, (c_eqm, 2 * (m + 1) + 1))
                    if i == 5 and there(u - 1):
                        bank_job([(c_oe, 1 + u)], [att_t[:, t * P:(t + 1) * P] for t in range(ST)], c_to, (c_eo, u))
                    if i == 7 and there(m + 1):
                        bank_job([], query_inputs(mj + 1, 1), c_tqm, (c_eqm, 2 * (m + 1) + 2))
                    if there(m):
                        for g in (2 * i, 2 * i + 1):
                            h, st = g // ST, g % ST
                            if g in (0, 8):
                                pe.wait_ge(c_eqm, 2 * m + g // 8 + 1)
                                pe.wait_ge(c_ek, 2 * (m + 1))
                            pe.wait_ge(c_red, 16 * m + g + 1)
                            nc.tensor.matmul(bank[g % 2], q_m[h // 2][:, st * P:(st + 1) * P],
                                             (k_lo, k_hi)[h % 2][mj % 4][:], start=True, stop=True).then_inc(c_mx, 1)
                    if there(u):
                        n = PAIRS * u + i
                        t, p = i // 2, i % 2
                        if i < 2:
                            pe.wait_ge(c_eqe, 2 * u + p + 1)
                        pe.wait_ge(c_e, n + 1)
                        for h in range(2):
                            last = nc.tensor.matmul(bank[2 + 2 * (i % 2) + h], (k_lo, k_hi)[h][j % 4][:, t * P:(t + 1) * P],
                                                    q_e[j % 2][p][:], start=True, stop=True)
                        last.then_inc(c_s, 1)
                    if i == 0 and there(u - 1):
                        attend(PAIRS * u - 1, PAIRS - 1, j - 1)
                    if i > 0 and there(u):
                        if i == 1:
                            pe.wait_ge(c_oe, u + 1)
                        attend(PAIRS * u + i - 1, i - 1, j)

            def phase_c():
                pe.wait_ge(c_const, 33)
                key_job(0, 0)
                for p in range(2):
                    bank_job([], query_inputs(0, p), c_tqm, (c_eqm, p + 1))
                slots(pe, attention)

            def phase_d():
                def logits(t):
                    pe.wait_ge(d_trs, t + 1)
                    for k in range(DC):
                        last = nc.tensor.matmul(bank[0][:, t * EXPERTS:(t + 1) * EXPERTS], xn_t[t % 2][:, k * P:(k + 1) * P],
                                                gw[:, k * EXPERTS:(k + 1) * EXPERTS], start=(k == 0), stop=(k == DC - 1))
                    last.then_inc(d_lg, 1)

                pe.wait_ge(ld_d, 4 * 16)
                for t in range(TILES):
                    pe.wait_ge(d_xn, t + 1)
                    if t >= 2:
                        pe.wait_ge(d_trs, t - 1)
                    for k in range(DC):
                        last = nc.tensor.transpose(bank[2 + t % 2][:, k * P:(k + 1) * P],
                                                   xn[:, t * D + k * P:t * D + (k + 1) * P], ident[:])
                    last.then_inc(d_tr, 1)
                    if t > 0:
                        logits(t - 1)
                logits(TILES - 1)
                pe.wait_ge(d_both, 1)
                n = TILES * EXPERTS
                nc.tensor.matmul(bank[1][:, 0:n], before[:], both[:], start=True, stop=True)
                nc.tensor.matmul(bank[1][:, n:2 * n], ones[:], both[:], start=True, stop=True).then_inc(d_rank, 1)

                def transpose_x(i, parity):
                    pe.wait_ge(e_ld[parity], 8 * (i - parity) + 16)
                    for k in range(DC):
                        last = nc.tensor.transpose(bank[4][:, k * P:(k + 1) * P], x_in[parity][:, k * P:(k + 1) * P], ident[:])
                    last.then_inc(e_xtr, 1)

                def down(i):
                    at = weights_column(i)
                    pe.wait_ge(e_ht0, i + 1)
                    pe.wait_ge(e_ht1, i + 1)
                    pe.wait_ge(e_y, i + 1)
                    for k in range(MOE // P):
                        last = nc.tensor.matmul(bank[7], h_dt[:, k * P:(k + 1) * P],
                                                w_all[:, bass.ds(at + 2 * DC * MOE + k * D, D)], start=(k == 0), stop=(k == MOE // P - 1))
                    last.then_inc(e_wo, 1)

                def weights_column(i):
                    return pe.value_load(plan[0:1, bass.ds(3 * i, 1)], min_val=0, max_val=EXPERT_COLS)

                def step(i, parity):
                    at = weights_column(i)
                    even = pe.value_load(plan[0:1, bass.ds(3 * i + 1, 1)], min_val=48, max_val=48 * EXPERTS)
                    odd = pe.value_load(plan[0:1, bass.ds(3 * i + 2, 1)], min_val=48, max_val=48 * EXPERTS)
                    pe.wait_ge(ld_w[0], even)
                    pe.wait_ge(ld_w[1], odd)
                    pe.wait_ge(e_xt, i + 1)
                    for half in range(2):
                        pe.wait_ge(e_h, 2 * i + half + 1)
                        for w in range(2):
                            for k in range(DC):
                                last = nc.tensor.matmul(bank[2 * half + w], x_t[parity][:, k * P:(k + 1) * P],
                                                        w_all[:, bass.ds(at + (w * DC + k) * MOE + half * 512, 512)],
                                                        start=(k == 0), stop=(k == DC - 1))
                        last.then_inc(e_gu, 1)
                    if not static(i) or i > 0:
                        down(i - 1)
                    if not static(i) or i + 1 < MTILES:
                        transpose_x(i + 1, 1 - parity)
                    for half in range(2):
                        pe.wait_ge(e_h, 2 * i + half + 3)
                        for k in range(4):
                            last = nc.tensor.transpose(bank[5 + half][:, k * P:(k + 1) * P],
                                                       h_d[:, (4 * half + k) * P:(4 * half + k + 1) * P], ident[:])
                        last.then_inc(e_htr, 1)

                pe.wait_ge(d_plan, 1)
                transpose_x(0, 0)
                tile_loop(pe, step)
                down(MTILES - 1)

            pe.sem_inc(e_xtr, 2)
            pe.sem_inc(e_wo, 1)
            pe.sem_inc(w_tp, 2)
            pe.sem_inc(b_tr, 1)
            pe.sem_inc(b_zc, 4)
            pe.sem_inc(c_tqe, 8)
            pe.sem_inc(c_tk, 2)
            pe.sem_inc(c_pv, 2)
            pe.wait_ge(ld_const, 5 * 16)
            context_t()
            pe.wait_ge(ctx_t_sb, BATCH + 1)
            with pe.Fori(0, BATCH) as b:
                phase_a(b)
            pe.wait_ge(pool_const, 4)
            weights()
            pe.wait_ge(had_ready, 1)
            with pe.Fori(0, BATCH) as b:
                phase_b(b)
            phase_c()
            phase_d()


def constants():
    h = np.ones((1, 1), np.float32)
    while h.shape[0] < D:
        h = np.block([[h, h], [h, -h]]).astype(np.float32)
    hadamard = h.reshape(DC, P, D).transpose(1, 0, 2).reshape(P, DC * D)
    before = np.triu(np.ones((P, P), np.float32), 1)
    routing = np.zeros((2, 512), np.float32)
    routing[0, :TILES * EXPERTS] = np.tile(EXPERTS - np.arange(EXPERTS), TILES)
    routing[1, :MTILES * EXPERTS] = np.repeat(np.arange(MTILES), EXPERTS)
    return {"c_ident": np.eye(P, dtype=np.float32), "c_hadamard": np.ascontiguousarray(hadamard, np.float32),
            "c_before": before, "c_routing": routing}


_INS = ["x", "ctx_512", "L0_xattn_W_k", "L0_xattn_b_k", "L0_xattn_ln_gamma", "L0_xattn_ln_beta", "L0_ffn_w_gate",
        "L0_ffn_w_up", "L0_ffn_w_down", "L1_ffn_gate_w", "L1_ffn_w0", "L1_ffn_w1", "L1_ffn_wo"]


def kernel(**inputs):
    import concourse.bacc as bacc
    from concourse.bass_utils import run_bass_kernel_spmd

    nc = bacc.Bacc("TRN2", target_bir_lowering=False, num_devices=1)
    arrays, args = {}, []
    for name, a in [(n, inputs[n]) for n in _INS] + list(constants().items()):
        a = np.ascontiguousarray(a)
        arrays[f"in_{name}"] = a
        args.append(nc.dram_tensor(f"in_{name}", a.shape, mybir.dt.from_np(a.dtype), kind="ExternalInput").ap())
    args.append(nc.dram_tensor("out", (BATCH, SEQ, D), F32, kind="ExternalOutput").ap())
    network(nc, *args)
    result = run_bass_kernel_spmd(nc, [arrays], core_ids=[0])
    return result.results[0]["out"]
```

```python
import math
from contextlib import ExitStack

import concourse.bass as bass
import numpy as np
from concourse import mybir

F32 = mybir.dt.float32
F32R = mybir.dt.float32r
BF16 = mybir.dt.bfloat16
I32 = mybir.dt.int32
ALU = mybir.AluOpType
ACT = mybir.ActivationFunctionType
AX = mybir.AxisListType

P = 128
BATCH, SEQ, D = 4, 512, 512
TILES = BATCH * SEQ // P
ST = SEQ // P
DC = D // P
CTX = 128
FF = 2048
FC = FF // P
HEADS, KVH, HD = 32, 8, 16
GROUP = HEADS // KVH
EXPERTS, MOE = 8, 1024
MTILES = 2 * TILES + EXPERTS - 1
ROWS = MTILES * P
EPS_SCORE, EPS_LN, EPS_Q = 1e-6, 1e-5, 1e-5
SCORE_SCALE = D ** -0.5
MAGIC = 1.5 * 2.0 ** 23
HAD_D, HAD_FF = 1.0 / math.sqrt(D), 1.0 / math.sqrt(FF)


class Count:

    def __init__(self, eng, sem, carrier=None):
        self.eng, self.sem, self.n, self.loops, self.carrier = eng, sem, 0, [], carrier

    def enter(self, i, per):
        self.loops.append((i, per, self.n))

    def leave(self, times):
        _, per, before = self.loops.pop()
        assert self.n - before == per, (self.n - before, per)
        self.n = before + per * times

    def inc(self, instruction):
        instruction.then_inc(self.sem, 1)
        self.n += 1

    def wait(self):
        value = self.n
        for i, per, _ in self.loops:
            value = value + i * per
        self.eng.wait_ge(self.sem, value)
        if self.carrier is not None:
            self.eng.sem_inc(self.carrier, 1)

    def step(self, instruction):
        self.inc(instruction)
        self.wait()


class Map:

    def __init__(self, nc, start, end):
        self.nc, self.start, self.at, self.end = nc, start, start, end

    def again(self):
        self.at = self.start

    def tile(self, name, shape, dtype=F32):
        size = int(np.prod(shape[1:])) * mybir.dt.size(dtype)
        t = self.nc.alloc_sbuf_tensor_at(name, list(shape), dtype, offset=self.at)
        self.at += (size + 31) // 32 * 32
        assert self.at <= self.end, (name, self.at - self.end)
        return t


def network(nc, x, ctx_512, w_k, b_k, ln_gamma, ln_beta, w_gate, w_up, w_down, gate_w, w0, w1, wo,
            c_ident, c_hadamard, c_before, c_routing, out):
    with ExitStack() as stack:
        def sem(name):
            return stack.enter_context(nc.semaphore(name))

        first = (nc.sbuf_base + 63) // 64 * 64
        keep = Map(nc, first, first + 37 * 1024)
        X = keep.tile("x_tiles", [P, TILES * D])
        ident = keep.tile("ident", [P, P])
        ident_b = keep.tile("ident_bf16", [P, P], BF16)
        st6 = keep.tile("ln_stats6", [P, ST * 6])
        mv = keep.tile("ln_mean_var", [P, ST * 2])
        var_eps = keep.tile("ln_var_eps", [P, ST])
        rstd = keep.tile("ln_rstd", [P, ST])
        half_neg = keep.tile("minus_half", [P, ST])
        magic = keep.tile("magic", [P, 1])
        ones = keep.tile("ones", [P, P])
        silu_first = keep.tile("silu_first", [P, 1])
        abs_sum = keep.tile("weight_abs_sum", [P, 3])
        w_mean = keep.tile("weight_scale", [P, 3])
        w_thr = keep.tile("weight_threshold", [P, 3])
        w_nthr = keep.tile("weight_neg_threshold", [P, 3])
        st6_all = keep.tile("stats6_all", [P, TILES * 6])
        mv_all = keep.tile("mean_var_all", [P, TILES * 2])
        ve_all = keep.tile("var_eps_all", [P, TILES])
        rstd_all = keep.tile("rstd_all", [P, TILES])
        half_neg_all = keep.tile("minus_half_all", [P, TILES])
        big = Map(nc, keep.end, keep.end + 112 * 1024)
        small = Map(nc, big.end, nc.sbuf_usable_end)
        first_small = small.start

        raw = [big.tile(f"raw_weight{i}", [P, FF * D // P]) for i in range(2)]
        wgu_t = [big.tile(f"{n}_ternary_t", [P, DC * FF], BF16) for n in ("gate", "up")]
        wd_t = big.tile("down_ternary_t", [P, FC * D], BF16)
        big.again()
        Y = big.tile("inner_t", [P, FC * SEQ])
        Z = big.tile("inner_half_rotated_t", [P, FC * SEQ])
        big.again()
        Y_lo = big.tile("inner_rotated_t_second", [P, FC * SEQ], F32R)
        Z_hi = big.tile("inner_rotated_t_first", [P, FC * SEQ], F32R)
        big.again()
        h_lo = big.tile("normed_tiles_t_second", [P, ST * D], F32R)

        neg = [small.tile(f"below_threshold{i}", [P, 512], BF16) for i in range(2)]
        tern = [small.tile(f"ternary_rows{i}", [P, 512], BF16) for i in range(2)]
        small.start = small.at

        a_p = small.tile("normed_tokens", [P, ST * D])
        a_pt = small.tile("normed_t", [P, DC * SEQ])
        ctx_t = small.tile("context_t", [CTX, BATCH * SEQ])
        kv_t = small.tile("kv_t", [CTX, SEQ])
        kv = small.tile("kv_tokens", [P, ST * CTX])
        o_t = small.tile("pair_product_t", [CTX, SEQ])
        gamma = small.tile("gamma_rows", [P, SEQ])
        beta = small.tile("beta_rows", [P, SEQ])
        wk_sb = small.tile("w_k", [CTX, CTX])
        wk_t = small.tile("w_k_t", [CTX, CTX])
        bk_col = small.tile("b_k_column", [CTX, 1])
        a_e = small.tile("score_exp", [P, ST * SEQ])
        a_mx = small.tile("score_neg_max", [P, ST])
        a_sum = small.tile("score_exp_sum", [P, ST])
        a_rs = small.tile("score_exp_rsum", [P, ST])
        keep_small = small.at
        a_z = small.tile("score_normed", [P, ST * SEQ])
        small.at = keep_small
        ctx_raw = small.tile("context_tokens", [P, TILES * CTX])

        small.again()
        h_b = small.tile("normed_or_scaled_tokens", [P, ST * D])
        here = small.at
        h_hi = small.tile("normed_tiles_t_first", [P, ST * D], F32R)
        small.at = here
        z_s = [small.tile("inner_rotated_rows0", [P, FF])]
        had = small.tile("hadamard", [P, DC * D], F32R)
        diag = small.tile("token_scale_diagonals", [P, ST * P])
        scale_rows = small.tile("token_scale_rows", [P, SEQ])
        q_b = small.tile("quantised_tokens", [P, FF], BF16)
        q_t = small.tile("quantised_t", [P, DC * SEQ], BF16)
        g_s = [small.tile(f"gate_scaled{i}", [P, SEQ]) for i in range(2)]
        g_silu = [small.tile(f"gate_silu{i}", [P, SEQ]) for i in range(2)]
        z_s.append(Map(nc, small.at - 4 * 4 * SEQ, small.at).tile("inner_rotated_rows1", [P, FF]))
        h_n = small.tile("normed_tokens_of_batch", [P, ST * D])
        q2_t = Map(nc, first_small, first_small + 4096).tile("inner_quantised_t", [P, FC * P], BF16)
        am = small.tile("abs_max", [P, ST])
        am_c = small.tile("abs_max_clipped", [P, ST])
        am_r = small.tile("abs_max_reciprocal", [P, ST])
        fac = small.tile("quantise_factor", [P, ST])
        tok_scale = small.tile("token_scale", [P, ST])
        inner_scale = small.tile("inner_scale", [P, ST])
        am2 = small.tile("inner_abs_max", [P, ST])
        am2_c = small.tile("inner_abs_max_clipped", [P, ST])
        am2_r = small.tile("inner_abs_max_reciprocal", [P, ST])
        fac2 = small.tile("inner_quantise_factor", [P, ST])
        deq = small.tile("inner_dequantise", [P, ST])

        small.start = first_small
        small.again()
        tail = Map(nc, big.end - 16 * 1024, big.end)
        ctx_c = tail.tile("context_tokens_again", [P, TILES * CTX])
        q_f = [small.tile(f"query_unit{i}", [P, ST * GROUP * HD]) for i in range(2)]
        q_s = [small.tile(f"query_parts{i}", [P, ST * GROUP * 64], F32R) for i in range(4)]
        k_s = [small.tile(f"key_parts_twice{i}", [P, ST * 2 * 64], F32R) for i in range(2)]
        v_u = [(keep if i < 4 else small).tile(f"value_and_one{i}", [P, ST * 32]) for i in range(8)]
        k_lo = [small.tile(f"key_t_first{i}", [P, SEQ], F32R) for i in range(4)]
        k_hi = [small.tile(f"key_t_second{i}", [P, SEQ], F32R) for i in range(4)]
        q_m = [small.tile(f"query_t_for_max{p}", [P, SEQ], F32R) for p in range(2)]
        q_e = [[small.tile(f"query_t_for_exp{i}{p}", [P, SEQ], F32R) for p in range(2)] for i in range(2)]
        prob = [tail.tile(f"probabilities{i}", [P, 2 * SEQ]) for i in range(2)]
        att_t = small.tile("attended_t", [P, SEQ])
        neg_max = [small.tile(f"neg_max{i}", [P, ST * GROUP]) for i in range(2)]
        att_r = small.tile("attended_rsum", [P, ST * GROUP])
        att_n = small.tile("attended_normed", [P, ST * GROUP * HD])

        zero_rows = small.tile("zero_rows", [P, D])

        BLOCK = DC * MOE
        w_r = Map(nc, first, small.end).tile("expert_weight_parts", [P, (small.start - first) // 4 + 2 * BLOCK], F32R)
        W_IN = [[(big.start - first) // 4, (big.start - first) // 4 + 2 * BLOCK],
                [0, (small.start - first) // 4]]
        WO_RAW = W_IN[0][1] + 2 * BLOCK
        WO = WO_RAW + BLOCK

        def block(name, column):
            at = first + 4 * column
            return Map(nc, at, at + 4 * BLOCK).tile(name, [P, BLOCK])

        w_in_raw = [[block(f"w{w}_of_{n}_expert", W_IN[p][w] + BLOCK) for w in range(2)] for p, n in enumerate(("even", "odd"))]
        wo_raw = block("wo_of_expert", WO_RAW)
        big.again()
        X2 = big.tile("x_tiles_again", [P, TILES * D])
        small.again()
        xn = small.tile("normed_all", [P, TILES * D])
        here = small.at
        x_in = [small.tile(f"sorted_tokens{i}", [P, D]) for i in range(2)]
        x_hi = small.tile("sorted_tokens_t_first", [P, D], F32R)
        x_lo = small.tile("sorted_tokens_t_second", [P, D], F32R)
        h_d = small.tile("expert_inner", [P, MOE])
        h_hi_d = small.tile("expert_inner_t_first", [P, MOE], F32R)
        h_lo_d = small.tile("expert_inner_t_second", [P, MOE], F32R)
        y_out = [small.tile(f"expert_out{i}", [P, D]) for i in range(2)]
        routed, small = small, Map(nc, here, small.at)
        xn_t = [small.tile(f"normed_all_t{i}", [P, D]) for i in range(4)]
        past_end = small.tile("past_end", [1, MTILES * EXPERTS])
        mt = {n: small.tile(f"tile_{n}", [1, MTILES]) for n in ("expert", "half", "parity")}
        mt_i = {n: small.tile(f"tilei_{n}", [1, MTILES], I32) for n in ("expert", "half")}
        gw = small.tile("router_weights", [P, DC * EXPERTS])
        before = small.tile("strictly_before", [P, P])
        num_e = small.tile("expert_numbers", [P, TILES * EXPERTS])
        num_tile = small.tile("tile_numbers", [1, MTILES * EXPERTS])
        lg = small.tile("logits", [P, TILES * EXPERTS])
        top = small.tile("logits_sorted", [P, TILES * EXPERTS])
        chosen = [small.tile(f"chosen{k}", [P, TILES * EXPERTS]) for k in range(2)]
        both = small.tile("chosen_either", [P, TILES * EXPERTS])
        running = small.tile("running_counts", [P, (TILES + 1) * EXPERTS])
        slot_e = small.tile("slot_by_expert", [P, TILES * EXPERTS])
        picked = [small.tile(f"slot_picked{k}", [P, TILES * EXPERTS]) for k in range(2)]
        slot_f = [small.tile(f"slot_f32_{k}", [P, TILES]) for k in range(2)]
        small = routed
        slot = [small.tile(f"slot{k}", [P, TILES], I32) for k in range(2)]
        gap = small.tile("logit_gap", [P, TILES])
        gap_e = small.tile("logit_gap_exp", [P, TILES])
        gap_1 = small.tile("softmax_sum", [P, TILES])
        top_w = [small.tile(f"top_weight{k}", [P, TILES]) for k in range(2)]
        row8 = {n: small.tile(f"experts_{n}", [P, EXPERTS]) for n in ("tiles", "end", "first")}
        row8_i = {n: small.tile(f"experts_{n}_int", [P, EXPERTS], I32) for n in ("count", "tiles", "wait")}
        plan = small.tile("tile_plan", [1, 3 * MTILES], I32)
        sorted_x = nc.dram_tensor("sorted_x", (ROWS, D), F32, kind="Internal").ap()
        sorted_y = nc.dram_tensor("sorted_y", (ROWS, D), F32, kind="Internal").ap()

        psum = stack.enter_context(nc.psum_tensor("psum", [P, 8 * 512], F32))
        bank = [psum[:, 512 * i:512 * i + 512] for i in range(8)]
        bank_b = [b.bitcast(BF16) for b in bank]

        def tiles(buf, i, n=1, width=D):
            return buf[:, bass.ds(i * width, n * width)]

        ld_const, ld_x, ld_ctx = sem("ld_const"), sem("ld_x"), sem("ld_ctx")
        ld_raw = [sem("ld_raw0"), sem("ld_raw1"), sem("ld_raw2")]
        stored = sem("stored")
        pool_const = sem("pool_const")
        dve_step, act_step, pool_step = sem("dve_step"), sem("act_step"), sem("pool_step")
        ctx_t_ps, ctx_t_sb = sem("ctx_t_ps"), sem("ctx_t_sb")
        ln_var, ln_rstd = sem("ln_var"), sem("ln_rstd")
        a_normed, a_trans, a_trans_sb = sem("a_normed"), sem("a_trans"), sem("a_trans_sb")
        a_kvt, a_kvt_sb, a_kv, a_kv_sb = sem("a_kvt"), sem("a_kvt_sb"), sem("a_kv"), sem("a_kv_sb")
        a_out, a_out_sb, a_sim, a_simz = sem("a_out"), sem("a_out_sb"), sem("a_sim"), sem("a_simz")
        a_zg, a_neg, a_exp, a_done = sem("a_zg"), sem("a_neg"), sem("a_exp"), sem("a_done")

        w_abs, w_tot = sem("w_abs"), sem("w_tot")
        w_tern, w_tp, w_evac = sem("w_tern"), sem("w_tp"), sem("w_evac")
        ld_had, had_ready = sem("ld_had"), sem("had_ready")
        b_normed, b_trans, b_trans_sb, b_fw, b_fac = sem("b_normed"), sem("b_trans"), sem("b_trans_sb"), sem("b_fw"), sem("b_fac")
        b_tq, b_q, b_qt, b_qts = sem("b_tq"), sem("b_q"), sem("b_qt"), sem("b_qts")
        b_dg, b_sps, b_sbc = sem("b_dg"), sem("b_sps"), sem("b_sbc")
        b_gp, b_up, b_g, b_sl, b_y, b_rot = sem("b_gp"), sem("b_up"), sem("b_g"), sem("b_sl"), sem("b_y"), sem("b_rot")
        b_lo, b_half, b_zhi, b_zlo, b_zlo0, b_zc = sem("b_lo"), sem("b_half"), sem("b_zhi"), sem("b_zlo"), sem("b_zlo0"), sem("b_zc")
        b_z, b_fac2, b_tq2, b_q2, b_tr, b_q2ts, b_dn, b_x = (sem("b_z"), sem("b_fac2"), sem("b_tq2"), sem("b_q2"),
                                                             sem("b_tr"), sem("b_q2ts"), sem("b_dn"), sem("b_x"))

        ld_ctx2, c_const, c_zero, c_var, c_rstd, c_prep = sem("ld_ctx2"), sem("c_const"), sem("c_zero"), sem("c_var"), sem("c_rstd"), sem("c_prep")
        c_tqe, c_tk, c_tqm, c_to = sem("c_tqe"), sem("c_tk"), sem("c_tqm"), sem("c_to")
        c_eqe, c_ek, c_eqm, c_eo = sem("c_eqe"), sem("c_ek"), sem("c_eqm"), sem("c_eo")
        c_mx, c_red, c_m, c_s, c_e, c_pv, c_oe = (sem("c_mx"), sem("c_red"), sem("c_m"), sem("c_s"), sem("c_e"),
                                                  sem("c_pv"), sem("c_oe"))

        c_x, pool_waited = sem("c_x"), sem("pool_waited")
        ld_d, ld_w, ld_wo = sem("ld_d"), [sem("ld_w_even"), sem("ld_w_odd")], sem("ld_wo")
        x_saved, x_back, w_in_parts, wo_parts = sem("x_saved"), sem("x_back"), sem("w_in_parts"), sem("wo_parts")
        d_xn, d_tr, d_trs, d_lg, d_both, d_rank, d_slot, d_gap, d_gap_e, d_plan = (
            sem("d_xn"), sem("d_tr"), sem("d_trs"), sem("d_lg"), sem("d_both"), sem("d_rank"), sem("d_slot"),
            sem("d_gap"), sem("d_gap_e"), sem("d_plan"))
        d_sc, d_zf, d_zero = sem("d_sc"), sem("d_zf"), sem("d_zero")
        e_ld, e_st = [sem("e_ld0"), sem("e_ld1")], [sem("e_st0"), sem("e_st1")]
        e_xtr, e_xh, e_xl, e_gu, e_silu, e_h, e_htr, e_hh, e_hl, e_wo, e_y = (
            sem("e_xtr"), sem("e_xh"), sem("e_xl"), sem("e_gu"), sem("e_silu"), sem("e_h"), sem("e_htr"), sem("e_hh"), sem("e_hl"),
            sem("e_wo"), sem("e_y"))
        d_got = [sem(f"d_got{i}") for i in range(8)]
        d_out = sem("d_out")

        def tile_loop(eng, step):
            step(0, 0)
            step(1, 1)
            step(2, 0)
            with eng.Fori(1, (MTILES - 3) // 2) as r:
                step(2 * r + 1, 1)
                step(2 * r + 2, 0)
            step(MTILES - 2, 1)
            step(MTILES - 1, 0)

        def token_tile(buf, st):
            return buf[:].rearrange("p (c n) -> p c n", c=FC)[:, :, st * P:(st + 1) * P]

        HALVES = slice(0, FC // 2), slice(FC // 2, FC)

        def static(i):
            return isinstance(i, int)
        UNITS = BATCH * KVH
        PAIRS = 2 * ST

        def slots(eng, slot, count=None, per=0):
            def bounded(v):
                return 0 <= v < UNITS
            for u in range(-2, KVH):
                slot(u, u % KVH, bounded)
            with eng.Fori(1, BATCH - 1) as b:
                if count:
                    count.enter(b - 1, per)
                for j in range(KVH):
                    slot(b * KVH + j, j, lambda v: True)
                if count:
                    count.leave(BATCH - 2)
            for u in range(UNITS - KVH, UNITS + 2):
                slot(u, u % KVH, bounded)

        block = stack.enter_context(nc.Block())

        @block.sync
        def _(sp):
            sp.dma_start(ident[:], c_ident).then_inc(ld_const, 16)
            sp.dma_start(ctx_raw[:].rearrange("p (t c) -> p t c", c=CTX),
                         ctx_512.rearrange("b (t p) c -> p (b t) c", p=P)).then_inc(ld_ctx, 16)
            sp.dma_start(wk_sb[:], w_k).then_inc(ld_const, 16)
            sp.dma_start(bk_col[:], b_k.rearrange("(p a) -> p a", a=1)).then_inc(ld_const, 16)
            sp.dma_start(gamma[:], ln_gamma.partition_broadcast(P)).then_inc(ld_const, 16)
            sp.dma_start(beta[:], ln_beta.partition_broadcast(P)).then_inc(ld_const, 16)
            sp.dma_start(X[:].rearrange("p (t c) -> p t c", c=D),
                         x.rearrange("b (t p) c -> p (b t) c", p=P)).then_inc(ld_x, 16)
            sp.dma_start(raw[0][:].rearrange("p (t c) -> p t c", c=D),
                         w_gate.rearrange("(t p) c -> p t c", p=P)).then_inc(ld_raw[0], 16)
            sp.dma_start(raw[1][:].rearrange("p (t c) -> p t c", c=D),
                         w_up.rearrange("(t p) c -> p t c", p=P)).then_inc(ld_raw[1], 16)
            sp.wait_ge(w_tern, FC)
            sp.wait_ge(w_abs, 1)
            sp.dma_start(raw[0][:].rearrange("p (t c) -> p t c", c=FF),
                         w_down.rearrange("(t p) c -> p t c", p=P)).then_inc(ld_raw[2], 16)
            sp.wait_ge(a_done, BATCH * ST)
            sp.dma_start(h_b[:], c_hadamard).then_inc(ld_had, 16)
            sp.wait_ge(b_x, BATCH * ST)
            sp.dma_start(ctx_c[:].rearrange("p (t c) -> p t c", c=CTX),
                         ctx_512.rearrange("b (t p) c -> p (b t) c", p=P)).then_inc(ld_ctx2, 16)

            def load_w_in(e, i):
                sp.dma_start(w_in_raw[e % 2][i][:].rearrange("p (k m) -> p k m", k=DC),
                             (w0, w1)[i][e, :, :].rearrange("(k p) m -> p k m", p=P)).then_inc(ld_w[e % 2], 16)

            def load_wo(e):
                sp.dma_start(wo_raw[:].rearrange("p (k m) -> p k m", k=MOE // P),
                             wo[e, :, :].rearrange("(k p) m -> p k m", p=P)).then_inc(ld_wo, 16)

            load_w_in(0, 0)
            load_w_in(0, 1)
            load_wo(0)
            sp.wait_ge(d_zero, 1)
            sp.dma_start(sorted_x.rearrange("(t p) c -> p t c", p=P),
                         zero_rows[:].rearrange("p (t c) -> p t c", t=1).broadcast_to([P, MTILES, D])).then_inc(d_zf, 16)
            sp.wait_ge(c_x, UNITS)
            sp.dma_start(gw[:].rearrange("p (k e) -> p k e", k=DC), gate_w.rearrange("(k p) e -> p k e", p=P)).then_inc(ld_d, 16)
            sp.dma_start(before[:], c_before).then_inc(ld_d, 16)
            n = TILES * EXPERTS
            sp.dma_start(num_e[:], c_routing[0, 0:n].partition_broadcast(P)).then_inc(ld_d, 16)
            sp.dma_start(num_tile[:], c_routing[1:2, 0:MTILES * EXPERTS]).then_inc(ld_d, 16)
            sp.wait_ge(d_xn, TILES)
            sp.dma_start(out.rearrange("b (t p) c -> p (b t) c", p=P), X[:].rearrange("p (t c) -> p t c", c=D)).then_inc(x_saved, 16)
            sp.wait_ge(x_saved, 16)
            load_w_in(1, 0)
            sp.wait_ge(d_sc, 2 * TILES * 16)
            load_w_in(1, 1)
            sp.wait_ge(wo_parts, 2)
            load_wo(1)
            sp.wait_ge(d_plan, 1)
            for e in range(2, EXPERTS + 1):
                end = sp.value_load(row8_i["wait"][0:1, e - 2:e - 1], min_val=1, max_val=MTILES + 1)
                sp.wait_ge(e_wo, end)
                if e < EXPERTS:
                    load_w_in(e, 0)
                    load_w_in(e, 1)
                    sp.wait_ge(wo_parts, 2 * e)
                    load_wo(e)
            sp.dma_start(X2[:].rearrange("p (t c) -> p t c", c=D), out.rearrange("b (t p) c -> p (b t) c", p=P)).then_inc(x_back, 16)
            for t in range(TILES):
                sp.wait_ge(d_out, 2 * t + 2)
                sp.dma_start(out[t // ST, (t % ST) * P:(t % ST + 1) * P, :], X2[:, t * D:(t + 1) * D]).then_inc(stored, 16)
            sp.wait_ge(stored, TILES * 16)

        @block.gpsimd
        def _(pool):
            nc.gpsimd.memset(half_neg[:], -0.5).then_inc(pool_const, 1)
            nc.gpsimd.memset(ones[:], 1.0).then_inc(pool_const, 1)
            nc.gpsimd.memset(magic[:], MAGIC).then_inc(pool_const, 1)
            c = Count(pool, pool_step, pool_waited)

            def inverse_root(n):
                pool.wait_ge(ln_var, n)
                nc.gpsimd.tensor_tensor(rstd[:], var_eps[:], half_neg[:], ALU.pow).then_inc(ln_rstd, 1)

            def phase_a(b):
                inverse_root(2 * b + 1)
                inverse_root(2 * b + 2)
                for st in range(ST):
                    pool.wait_ge(a_simz, b * ST + st + 1)
                    z = a_z[:, st * SEQ:(st + 1) * SEQ]
                    c.step(nc.gpsimd.tensor_tensor(z, z, gamma[:], ALU.mult))
                    nc.gpsimd.tensor_tensor(z, z, beta[:], ALU.add).then_inc(a_zg, 1)

            def phase_b(b):
                for a in range(2):
                    with pool.Fori(0, 4) as i:
                        pool.wait_ge(b_y, 2 + b * FC + a * 8 + 2 * i + 2)
                        pool.sem_inc(pool_waited, 1)
                        y0, y1 = (Y[:, bass.ds((8 * a + i + 4 * h) * SEQ, SEQ)] for h in range(2))
                        nc.gpsimd.tensor_tensor(Z[:, bass.ds((8 * a + i) * SEQ, SEQ)], y0, y1, ALU.add).then_inc(b_half, 1)
                        nc.gpsimd.tensor_tensor(Z[:, bass.ds((8 * a + i + 4) * SEQ, SEQ)], y0, y1, ALU.subtract).then_inc(b_half, 1)
                for st in range(1, ST):
                    pool.wait_ge(b_zhi, b * (ST + 1) + 2 + st)
                    pool.sem_inc(pool_waited, 1)
                    nc.gpsimd.tensor_tensor(token_tile(Y_lo, st), token_tile(Y, st), token_tile(Z_hi, st),
                                            ALU.subtract).then_inc(b_zlo, 1)

            def phase_c(c):
                nc.gpsimd.memset(half_neg_all[:], -0.5).then_inc(c_const, 1)
                pool.wait_ge(b_x, BATCH * ST)
                for v in v_u:
                    nc.gpsimd.memset(v[:], 0.0).then_inc(c_const, 1)
                pool.wait_ge(c_const, 1 + 8)
                for v in v_u:
                    nc.gpsimd.memset(v[:].rearrange("p (t c) -> p t c", c=32)[:, :, HD:HD + 1], 1.0).then_inc(c_const, 1)
                pool.wait_ge(c_const, 1 + 8 + 8)
                pool.wait_ge(c_var, 1)
                nc.gpsimd.tensor_tensor(rstd_all[:], ve_all[:], half_neg_all[:], ALU.pow).then_inc(c_rstd, 1)
                pool.wait_ge(c_zero, 6)
                for k in k_s:
                    nc.gpsimd.memset(k[:].bitcast(F32).rearrange("p (t c) -> p t c", c=64)[:, :, 48:50], 1.0).then_inc(c_const, 1)
                pool.wait_ge(c_const, 1 + 8 + 8 + 2)
                nc.gpsimd.memset(zero_rows[:], 0.0).then_inc(d_zero, 1)
                pool.wait_ge(c_rstd, 1)
                pool.wait_ge(ld_ctx2, 16)
                with pool.Fori(0, BATCH) as b:
                    c.enter(b, KVH * 7)
                    for j in range(KVH):
                        unit_parts(c, b, j)
                    c.leave(BATCH)

            def phase_d():
                w_in_split(0, 0)
                pool.wait_ge(c_x, UNITS)
                pool.wait_ge(c_var, 2)
                nc.gpsimd.tensor_tensor(rstd_all[:], ve_all[:], half_neg_all[:], ALU.pow).then_inc(c_rstd, 1)
                w_in_split(0, 1)
                wo_split(0)
                pool.wait_ge(d_zf, 16)
                pool.wait_ge(d_slot, 2)
                pool.wait_ge(d_xn, TILES)
                for t in range(TILES):
                    for k in range(2):
                        pool.indirect_dma_start(out=sorted_x, out_offset=bass.IndirectOffsetOnAxis(ap=slot[k][:, t:t + 1], axis=0),
                                                in_=xn[:, t * D:(t + 1) * D], in_offset=None).then_inc(d_sc, 16)
                pool.wait_ge(d_sc, 2 * TILES * 16)

                pool.wait_ge(d_plan, 1)
                for e in range(1, EXPERTS):
                    w_in_split(e, 0)
                    w_in_split(e, 1)
                    end = pool.value_load(row8_i["wait"][0:1, e - 1:e], min_val=1, max_val=MTILES + 1)
                    pool.wait_ge(e_wo, end)
                    pool.sem_inc(pool_waited, 1)
                    wo_split(e)
                pool.wait_ge(e_st[0], 16 * ((MTILES + 1) // 2))
                pool.wait_ge(e_st[1], 16 * (MTILES // 2))
                for t in range(TILES):
                    if t >= 8:
                        pool.wait_ge(d_out, 2 * (t - 8) + 2)
                    for k in range(2):
                        pool.indirect_dma_start(out=xn[:, (2 * t + k) % 16 * D:((2 * t + k) % 16 + 1) * D], out_offset=None,
                                                in_=sorted_y,
                                                in_offset=bass.IndirectOffsetOnAxis(ap=slot[k][:, t:t + 1], axis=0)).then_inc(d_got[t % 8], 16)

            def split(raw, hi, lo, done, halves=False):
                for h in range(2):
                    s = h * BLOCK // 2
                    w = raw[:, s:s + BLOCK // 2]
                    first_part = w_r[:, hi + s:hi + s + BLOCK // 2]
                    c.step(nc.gpsimd.tensor_tensor(first_part, w, ones[:, 0:1].broadcast_to([P, BLOCK // 2]), ALU.mult))
                    last = nc.gpsimd.tensor_tensor(w_r[:, lo + s:lo + s + BLOCK // 2], w, first_part, ALU.subtract)
                    if halves or h == 1:
                        last.then_inc(done, 1)

            def w_in_split(e, i):
                pool.wait_ge(ld_w[e % 2], 32 * (e // 2 + 1))
                pool.sem_inc(pool_waited, 1)
                at = W_IN[e % 2][i]
                split(w_in_raw[e % 2][i], at, at + BLOCK, w_in_parts)

            def wo_split(e):
                pool.wait_ge(ld_wo, 16 * (e + 1))
                pool.sem_inc(pool_waited, 1)
                split(wo_raw, WO, WO + BLOCK, wo_parts, halves=True)

            def unit_parts(c, b, j):
                u = b * KVH + j
                f = q_f[j % 2][:].rearrange("p (t c) -> p t c", t=ST)
                fh = q_f[j % 2][:].rearrange("p (n c) -> p n c", c=HD)
                qs = q_s[j % 4][:].rearrange("p (n c) -> p n c", c=64)
                ks = k_s[j % 2][:].rearrange("p (t a c) -> p t a c", a=2, c=64)
                xs = tiles(X, b * ST, ST).rearrange("p (t c) -> p t c", c=D)[:, :, j * 64:(j + 1) * 64]
                mean = mv_all[:, bass.ds(b * 2 * ST, 2 * ST)].rearrange("p (t c) -> p t c", c=2)[:, :, 0:1]
                r = rstd_all[:, bass.ds(b * ST, ST)].rearrange("p (t c) -> p t c", c=1)
                cx = tiles(ctx_c, b * ST, ST, CTX).rearrange("p (t c) -> p t c", c=CTX)[:, :, j * HD:(j + 1) * HD]
                cx2 = cx.rearrange("p t (a c) -> p t a c", a=1).broadcast_to([P, ST, 2, HD])
                pool.wait_ge(c_tk, u + 1)
                pool.wait_ge(c_tqe, 2 * u + 2)
                pool.sem_inc(pool_waited, 1)
                c.step(nc.gpsimd.tensor_tensor(f, xs, mean.broadcast_to([P, ST, 64]), ALU.subtract))
                c.step(nc.gpsimd.tensor_tensor(f, f, r.broadcast_to([P, ST, 64]), ALU.mult))
                c.inc(nc.gpsimd.tensor_copy(qs[:, :, 0:HD], fh))
                c.inc(nc.gpsimd.tensor_copy(ks[:, :, :, 0:HD], cx2))
                c.step(nc.gpsimd.tensor_copy(v_u[j % 8][:].rearrange("p (t c) -> p t c", c=32)[:, :, 0:HD], cx))
                c.inc(nc.gpsimd.tensor_copy(qs[:, :, 2 * HD:3 * HD], fh))
                c.inc(nc.gpsimd.tensor_copy(ks[:, :, :, HD:2 * HD], cx2))
                nc.gpsimd.memset(qs[:, :, 48:50].bitcast(F32), 0.0).then_inc(c_prep, 1)
                nc.gpsimd.tensor_tensor(qs[:, :, HD:2 * HD], fh, qs[:, :, 0:HD], ALU.subtract).then_inc(c_prep, 1)
                nc.gpsimd.tensor_tensor(ks[:, :, :, 2 * HD:3 * HD], cx2, ks[:, :, :, 0:HD], ALU.subtract).then_inc(c_prep, 1)

            pool.wait_ge(pool_const, 3)
            pool.wait_ge(ld_const, 5 * 16)
            nc.gpsimd.tensor_copy(ident_b[:], ident[:]).then_inc(pool_const, 1)
            with pool.Fori(0, BATCH) as b:
                c.enter(b, ST)
                phase_a(b)
                c.leave(BATCH)
            inverse_root(2 * BATCH + 1)
            with pool.Fori(0, BATCH - 1) as b:
                phase_b(b)
                inverse_root(2 * BATCH + b + 2)
            phase_b(BATCH - 1)
            phase_c(c)
            phase_d()

        @block.scalar
        def _(act):
            def context_t():
                for b in range(BATCH):
                    act.wait_ge(ctx_t_ps, b + 1)
                    nc.scalar.activation(ctx_t[:, b * SEQ:(b + 1) * SEQ], bank[b], ACT.Copy).then_inc(ctx_t_sb, 1)
                act.wait_ge(ctx_t_ps, BATCH + 1)
                nc.scalar.activation(wk_t[:], bank[4][:, 0:CTX], ACT.Copy).then_inc(ctx_t_sb, 1)

            def phase_a(b):
                act.wait_ge(a_kvt, b + 1)
                nc.scalar.activation(kv_t[:], bank[2], ACT.Identity, bias=bk_col[:, 0:1]).then_inc(a_kvt_sb, 1)
                for st in range(ST):
                    act.wait_ge(a_trans, b * ST + st + 1)
                    nc.scalar.activation(
                        a_pt[:].rearrange("p (k n) -> p k n", k=DC)[:, :, st * P:(st + 1) * P],
                        bank[st % 2].rearrange("p (k n) -> p k n", k=DC), ACT.Copy).then_inc(a_trans_sb, 1)
                weight_rows(b, 0, 2)
                act.wait_ge(a_kv, b + 1)
                nc.scalar.activation(kv[:], bank[2], ACT.Copy).then_inc(a_kv_sb, 1)
                weight_rows(b, 2, 4)
                act.wait_ge(a_out, b + 1)
                nc.scalar.activation(o_t[:], bank[2], ACT.Copy).then_inc(a_out_sb, 1)
                weight_rows(b, 4, 8)
                if b < 3:
                    weight_abs(b)
                weight_rows(b, 8, 13)
                for st in range(ST):
                    act.wait_ge(a_neg, b * ST + st + 1)
                    nc.scalar.activation(a_e[:, st * SEQ:(st + 1) * SEQ], a_z[:, st * SEQ:(st + 1) * SEQ], ACT.Exp,
                                         bias=a_mx[:, st:st + 1], accum_out=a_sum[:, st:st + 1]).then_inc(a_exp, 1)
                weight_rows(b, 13, FC)

            def weight_abs(w):
                act.wait_ge(ld_raw[w], 16)
                if w:
                    act.wait_ge(w_abs, w)
                nc.scalar.activation(wd_t[:], raw[w % 2][:], ACT.Abs, accum_out=abs_sum[:, w:w + 1]).then_inc(w_abs, 1)

            def weight_rows(b, start, end):
                for u in range(start, end if b else start):
                    w = b - 1
                    if w < 2:
                        place = wgu_t[w][:].rearrange("p (k f) -> p k f", k=DC)[:, :, u * P:(u + 1) * P]
                    else:
                        hc, q = u // 4, u % 4
                        place = wd_t[:].rearrange("p (f h) -> p f h", f=FC)[:, 4 * q:4 * q + 4, hc * P:(hc + 1) * P]
                    act.wait_ge(w_tp, 2 + w * FC + u + 1)
                    nc.scalar.activation(place, t_view(3), ACT.Copy).then_inc(w_evac, 1)

            def t_view(n):
                return bank_b[n][:, 0:512].rearrange("p (k n) -> p k n", k=4)

            def phase_b(b):
                for st in range(ST):
                    act.wait_ge(b_trans, b * ST + st + 1)
                    nc.scalar.activation(h_hi[:, st * D:(st + 1) * D], bank[st % 2], ACT.Copy).then_inc(b_trans_sb, 1)
                act.wait_ge(b_fac, b + 1)
                for st in range(ST):
                    nc.scalar.activation(h_b[:, st * D:(st + 1) * D], bank[4 + st], ACT.Identity,
                                         bias=magic[:, 0:1], scale=fac[:, st:st + 1]).then_inc(b_tq, 1)
                act.wait_ge(b_sps, b + 1)
                nc.scalar.activation(scale_rows[:], bank[0], ACT.Copy).then_inc(b_sbc, 1)
                for a in range(2):
                    with act.Fori(0, 4) as i:
                        for h in range(2):
                            n = b * FC + a * 8 + 2 * i + h
                            act.wait_ge(b_g, 2 + n + 1)
                            act.wait_ge(b_y, n + 1)
                            nc.scalar.activation(g_silu[h][:], g_s[h][:], ACT.Silu, scale=w_mean[:, 0:1]).then_inc(b_sl, 1)

                def first_part(st):
                    if st == 0:
                        for h, half in enumerate(HALVES):
                            act.wait_ge(b_rot, 2 * b * ST + h + 1)
                            if h == 0:
                                act.wait_ge(b_rot, 2 * b * ST + 2)
                            nc.scalar.activation(token_tile(Z_hi, st)[:, half], token_tile(Y, st)[:, half], ACT.Copy).then_inc(b_zhi, 1)
                        return
                    act.wait_ge(b_rot, 2 * (b * ST + st) + 2)
                    nc.scalar.activation(token_tile(Z_hi, st), token_tile(Y, st), ACT.Copy).then_inc(b_zhi, 1)

                def transposed(n):
                    act.wait_ge(b_tr, 1 + n + 1)
                    nc.scalar.activation(q2_t[:], psum[:, 0:1024].bitcast(BF16), ACT.Copy).then_inc(b_q2ts, 1)

                first_part(0)
                first_part(1)
                act.wait_ge(b_y, 2 + (b + 1) * FC)
                for st in range(ST):
                    n = b * ST + st
                    if st >= 2:
                        act.wait_ge(b_tq2, 1 + n - 1)
                    for g in range(4):
                        if g == 3 and st > 0:
                            transposed(n - 1)
                        act.wait_ge(b_z, 4 * n + g + 1)
                        nc.scalar.activation(z_s[st % 2][:, g * D:(g + 1) * D], bank[4 + g], ACT.Copy).then_inc(b_zc, 1)
                    act.wait_ge(b_fac2, n + 1)
                    act.wait_ge(b_q2, n + 1)
                    nc.scalar.activation(h_b[:], z_s[st % 2][:], ACT.Identity, bias=magic[:, 0:1],
                                         scale=fac2[:, st:st + 1]).then_inc(b_tq2, 1)
                    if st + 2 < ST:
                        first_part(st + 2)
                transposed(b * ST + ST - 1)

            def attention(u, j, there):
                m, mj = u + 2, (j + 2) % 8

                def evac_parts(out, job, n, done):
                    act.wait_ge(job, n)
                    nc.scalar.activation(out[:], bank[7], ACT.Copy).then_inc(done, 1)

                for i in range(PAIRS):
                    if i in (1, 2) and there(m - 1):
                        p = i - 1
                        evac_parts(q_e[(mj + 1) % 2][p], c_tqe, 8 + 2 * (m - 1) + p + 1, c_eqe)
                    if i == 3 and there(m + 1):
                        r = (mj + 1) % 4
                        act.wait_ge(c_tk, 2 + m + 2)
                        nc.scalar.activation(k_lo[r][0:64, :], bank[7][0:64, :], ACT.Copy).then_inc(c_ek, 1)
                        nc.scalar.activation(k_hi[r][64:P, :], bank[7][64:P, :], ACT.Copy).then_inc(c_ek, 1)
                    if i == 4 and there(m + 1):
                        evac_parts(q_m[0], c_tqm, 2 * (m + 1) + 1, c_eqm)
                    if there(u):
                        n = PAIRS * u + i
                        act.wait_ge(c_s, n + 1)
                        act.wait_ge(c_pv, n + 1)
                        nc.scalar.activation(prob[i % 2][:], psum[:, (2 + 2 * (i % 2)) * 512:(4 + 2 * (i % 2)) * 512], ACT.Exp,
                                             scale=HD ** -0.5).then_inc(c_e, 1)
                if there(m + 1):
                    if there(m):
                        act.wait_ge(c_mx, 16 * (m + 1))
                    evac_parts(q_m[1], c_tqm, 2 * (m + 1) + 2, c_eqm)

            def phase_d():
                for t in range(TILES):
                    act.wait_ge(d_tr, t + 1)
                    if t >= 4:
                        act.wait_ge(d_lg, t - 3)
                    nc.scalar.activation(xn_t[t % 4][:], bank[2 + t % 4], ACT.Copy).then_inc(d_trs, 1)
                act.wait_ge(d_gap, 1)
                nc.scalar.activation(gap_e[:], gap[:], ACT.Exp).then_inc(d_gap_e, 1)

                def load(i, parity):
                    act.wait_ge(e_xtr, i + 1)
                    nc.scalar.dma_start(x_in[parity][:], sorted_x[bass.ds(i * P, P), :]).then_inc(e_ld[parity], 16)

                def store(i, parity):
                    act.wait_ge(e_y, i + 2)
                    nc.scalar.dma_start(sorted_y[bass.ds(i * P, P), :], y_out[parity][:]).then_inc(e_st[parity], 16)

                def x_first(i):
                    act.wait_ge(e_xtr, 2 + i + 1)
                    nc.scalar.activation(x_hi[:], bank[4], ACT.Copy).then_inc(e_xh, 1)

                def step(i, parity):
                    if not static(i) or i + 2 < MTILES:
                        load(i + 2, parity)
                    for half in range(2):
                        act.wait_ge(e_gu, 2 * i + half + 1)
                        act.wait_ge(e_htr, 2 * i + half + 1)
                        nc.scalar.activation(h_d[:, half * 512:(half + 1) * 512], bank[2 * half], ACT.Silu).then_inc(e_silu, 1)
                    if not static(i) or i + 1 < MTILES:
                        x_first(i + 1)
                    for half in range(2):
                        act.wait_ge(e_htr, 2 + 2 * i + half + 1)
                        nc.scalar.activation(h_hi_d[:, half * 512:(half + 1) * 512], bank[5 + half], ACT.Copy).then_inc(e_hh, 1)
                    if not static(i) or i > 0:
                        store(i - 1, 1 - parity)

                act.wait_ge(d_sc, 2 * TILES * 16)
                load(0, 0)
                load(1, 1)
                x_first(0)
                tile_loop(act, step)
                store(MTILES - 1, 0)

            def phase_c():
                act.wait_ge(c_zero, 6 + 8)
                act.wait_ge(c_tk, 2 + 1)
                nc.scalar.activation(k_lo[0][0:64, :], bank[7][0:64, :], ACT.Copy).then_inc(c_ek, 1)
                nc.scalar.activation(k_hi[0][64:P, :], bank[7][64:P, :], ACT.Copy).then_inc(c_ek, 1)
                for p in range(2):
                    act.wait_ge(c_tqm, p + 1)
                    nc.scalar.activation(q_m[p][:], bank[7], ACT.Copy).then_inc(c_eqm, 1)
                slots(act, attention)

            act.sem_inc(b_tq2, 1)
            act.wait_ge(ld_const, 5 * 16)
            act.wait_ge(pool_const, 4)
            context_t()
            for b in range(BATCH):
                phase_a(b)
            nc.scalar.activation(silu_first[:], magic[:], ACT.Silu).then_inc(act_step, 1)
            act.wait_ge(ld_had, 16)
            nc.scalar.activation(had[:], h_b[:], ACT.Copy).then_inc(had_ready, 1)
            with act.Fori(0, BATCH) as b:
                phase_b(b)
            act.sem_inc(c_e, 2)
            phase_c()
            phase_d()

        @block.vector
        def _(dve):
            c = Count(dve, dve_step)

            def layer_norm(b, out_tiles, group, written):
                norm_statistics(b)
                norm_tokens(b, out_tiles, group, written)

            def norm_statistics(b):
                for st in range(ST):
                    c.inc(nc.vector.bn_stats(st6[:, 6 * st:6 * st + 6], tiles(X, b * ST + st)))
                c.wait()
                c.inc(nc.vector.memset(var_eps[:, 0:1], 1.0))
                for st in range(ST):
                    c.inc(nc.vector.bn_aggr(mv[:, 2 * st:2 * st + 2], st6[:, 6 * st:6 * st + 6]))
                c.wait()
                nc.vector.tensor_scalar(var_eps[:], mv[:, 1:2 * ST:2], 1.0, EPS_LN, ALU.mult, ALU.add).then_inc(ln_var, 1)

            def norm_tokens(b, out_tiles, group, written):
                dve.wait_ge(ln_rstd, group)
                for st in range(ST):
                    nc.vector.tensor_scalar(out_tiles[:, st * D:(st + 1) * D], tiles(X, b * ST + st),
                                            mv[:, 2 * st:2 * st + 1], rstd[:, st:st + 1],
                                            ALU.subtract, ALU.mult).then_inc(written, 1)

            def phase_a(b):
                weight_rows(b, 0, 8)
                dve.wait_ge(a_sim, b * ST + ST)
                for st in range(ST):
                    c.inc(nc.vector.bn_stats(st6[:, 6 * st:6 * st + 6], bank[4 + st]))
                c.wait()
                c.inc(nc.vector.memset(var_eps[:, 0:1], 1.0))
                for st in range(ST):
                    c.inc(nc.vector.bn_aggr(mv[:, 2 * st:2 * st + 2], st6[:, 6 * st:6 * st + 6]))
                c.wait()
                nc.vector.tensor_scalar(var_eps[:], mv[:, 1:2 * ST:2], SCORE_SCALE ** 2, EPS_SCORE,
                                        ALU.mult, ALU.add).then_inc(ln_var, 1)
                dve.wait_ge(ln_rstd, 2 * b + 2)
                c.step(nc.vector.tensor_scalar(a_rs[:], rstd[:], SCORE_SCALE, None, ALU.mult))
                for st in range(ST):
                    nc.vector.tensor_scalar(a_z[:, st * SEQ:(st + 1) * SEQ], bank[4 + st],
                                            mv[:, 2 * st:2 * st + 1], a_rs[:, st:st + 1],
                                            ALU.subtract, ALU.mult).then_inc(a_simz, 1)
                weight_rows(b, 8, 13)
                for st in range(ST):
                    dve.wait_ge(a_zg, b * ST + st + 1)
                    nc.vector.tensor_reduce(a_mx[:, st:st + 1], a_z[:, st * SEQ:(st + 1) * SEQ], AX.X, ALU.max,
                                            negate=True).then_inc(a_neg, 1)
                if b + 1 < BATCH:
                    layer_norm(b + 1, a_p, 2 * b + 3, a_normed)
                weight_rows(b, 13, FC)
                dve.wait_ge(a_exp, b * ST + ST)
                c.step(nc.vector.reciprocal(a_rs[:], a_sum[:]))
                for st in range(ST):
                    xt = tiles(X, b * ST + st)
                    nc.vector.scalar_tensor_tensor(out=xt, in0=a_e[:, st * SEQ:(st + 1) * SEQ], scalar=a_rs[:, st:st + 1],
                                                   in1=xt, op0=ALU.mult, op1=ALU.add).then_inc(a_done, 1)
                if b < 3:
                    weight_scale(b)

            def weight_scale(w):
                dve.wait_ge(w_tot, w + 1)
                c.step(nc.vector.tensor_scalar(w_mean[:, w:w + 1], bank[3][:, w:w + 1], 1.0 / (FF * D), EPS_Q, ALU.mult, ALU.max))
                c.inc(nc.vector.tensor_scalar(w_thr[:, w:w + 1], w_mean[:, w:w + 1], 0.5, None, ALU.mult))
                c.step(nc.vector.tensor_scalar(w_nthr[:, w:w + 1], w_mean[:, w:w + 1], -0.5, None, ALU.mult))

            def ternary(w, unit, src, h):
                dve.wait_ge(w_tp, unit + 1)
                c.step(nc.vector.tensor_scalar(neg[h][:], src, w_nthr[:, w:w + 1], None, ALU.is_lt))
                nc.vector.scalar_tensor_tensor(out=tern[h][:], in0=src, scalar=w_thr[:, w:w + 1], in1=neg[h][:],
                                               op0=ALU.is_gt, op1=ALU.subtract).then_inc(w_tern, 1)

            def weight_rows(b, start, end):
                for u in range(start, end if b else start):
                    w = b - 1
                    ternary(w, w * FC + u, raw[w % 2][:, u * 512:(u + 1) * 512], u % 2)

            def phase_b(b, more):
                for st in range(ST):
                    dve.wait_ge(b_trans_sb, b * ST + st + 1)
                    nc.vector.tensor_tensor(h_lo[:, st * D:(st + 1) * D], bank[st % 2], h_hi[:, st * D:(st + 1) * D],
                                            ALU.subtract).then_inc(b_lo, 1)
                for st in range(ST):
                    dve.wait_ge(b_fw, b * ST + st + 1)
                    c.inc(nc.vector.tensor_reduce(am[:, st:st + 1], bank[4 + st], AX.X, ALU.max, apply_absolute_value=True))
                c.wait()
                c.step(nc.vector.tensor_scalar(am_c[:], am[:], HAD_D, EPS_Q, ALU.mult, ALU.max))
                c.inc(nc.vector.tensor_scalar(tok_scale[:], am_c[:], 1.0 / 127.0, None, ALU.mult))
                c.step(nc.vector.reciprocal(am_r[:], am_c[:]))
                nc.vector.tensor_scalar(fac[:], am_r[:], 127.0 * HAD_D, None, ALU.mult).then_inc(b_fac, 1)
                for st in range(ST):
                    last = nc.vector.tensor_scalar(diag[:, st * P:(st + 1) * P], ident[:], tok_scale[:, st:st + 1], None, ALU.mult)
                last.then_inc(b_dg, 1)
                c.step(nc.vector.tensor_scalar(inner_scale[:], tok_scale[:], w_mean[:, 1:2], HAD_FF, ALU.mult, ALU.mult))
                for st in range(ST):
                    dve.wait_ge(b_tq, b * ST + st + 1)
                    nc.vector.tensor_scalar(q_b[:, st * D:(st + 1) * D], h_b[:, st * D:(st + 1) * D], MAGIC, 127.0,
                                            ALU.subtract, ALU.min).then_inc(b_q, 1)
                for st in range(ST):
                    dve.wait_ge(b_qt, b * ST + st + 1)
                    nc.vector.tensor_copy(q_t[:].rearrange("p (k n) -> p k n", k=DC)[:, :, st * P:(st + 1) * P],
                                          bank_b[2 + st % 2][:, 0:512].rearrange("p (k n) -> p k n", k=DC)).then_inc(b_qts, 1)
                for a in range(2):
                    with dve.Fori(0, 4) as i:
                        n = b * FC + a * 8 + 2 * i
                        dve.wait_ge(b_sbc, b + 1)
                        for h in range(2):
                            dve.wait_ge(b_gp, n + h + 1)
                            nc.vector.tensor_tensor(g_s[h][:], bank[h], scale_rows[:], ALU.mult).then_inc(b_g, 1)
                        for h in range(2):
                            dve.wait_ge(b_sl, n + h + 1)
                            dve.wait_ge(b_up, n + h + 1)
                            nc.vector.tensor_tensor(Y[:, bass.ds((8 * a + i + 4 * h) * SEQ, SEQ)], bank[2 + h], g_silu[h][:],
                                                    ALU.mult).then_inc(b_y, 1)

                def second_stage(st):
                    x0, x1 = token_tile(Z, st)[:, 0:8], token_tile(Z, st)[:, 8:16]
                    nc.vector.tensor_tensor(token_tile(Y, st)[:, 0:8], x0, x1, ALU.add).then_inc(b_rot, 1)
                    nc.vector.tensor_tensor(token_tile(Y, st)[:, 8:16], x0, x1, ALU.subtract).then_inc(b_rot, 1)

                dve.wait_ge(b_half, (b + 1) * FC)
                second_stage(0)
                for h, half in enumerate(HALVES):
                    dve.wait_ge(b_zhi, b * (ST + 1) + h + 1)
                    nc.vector.tensor_tensor(token_tile(Y_lo, 0)[:, half], token_tile(Y, 0)[:, half], token_tile(Z_hi, 0)[:, half],
                                            ALU.subtract).then_inc(b_zlo0, 1)
                second_stage(1)
                for st in range(ST + 1):
                    n = b * ST + st
                    if st < ST:
                        s = slice(st, st + 1)
                        dve.wait_ge(b_zc, 4 + 4 * (n + 1))
                        c.step(nc.vector.tensor_reduce(am2[:, s], z_s[st % 2][:], AX.X, ALU.max, apply_absolute_value=True))
                        c.step(nc.vector.tensor_scalar(am2_c[:, s], am2[:, s], inner_scale[:, s], EPS_Q, ALU.mult, ALU.max))
                        c.inc(nc.vector.tensor_scalar(deq[:, s], am2_c[:, s], w_mean[:, 2:3], 1.0 / 127.0, ALU.mult, ALU.mult))
                        c.step(nc.vector.reciprocal(am2_r[:, s], am2_c[:, s]))
                        nc.vector.tensor_scalar(fac2[:, s], am2_r[:, s], inner_scale[:, s], 127.0, ALU.mult, ALU.mult).then_inc(b_fac2, 1)
                        if st + 2 < ST:
                            second_stage(st + 2)
                        dve.wait_ge(b_tq2, 1 + n + 1)
                        dve.wait_ge(b_tr, n + 1)
                        nc.vector.tensor_scalar(q_b[:], h_b[:], MAGIC, 127.0, ALU.subtract, ALU.min).then_inc(b_q2, 1)
                    if st > 0:
                        dve.wait_ge(b_dn, n)
                        xt = tiles(X, n - 1)
                        nc.vector.scalar_tensor_tensor(out=xt, in0=bank[2 + (st - 1) % 2], scalar=deq[:, st - 1:st], in1=xt,
                                                       op0=ALU.mult, op1=ALU.add).then_inc(b_x, 1)
                        dve.wait_ge(b_x, n)
                        if more and st == 2:
                            norm_statistics(b + 1)
                        if more and st == 3:
                            norm_tokens(b + 1, h_n, 2 * BATCH + b + 2, b_normed)
                        c.inc(nc.vector.bn_stats(st6_all[:, bass.ds(6 * (n - 1), 6)], xt))

            def attention(u, j, there):
                m, mj = u + 2, (j + 2) % 8
                for i in range(PAIRS):
                    if i == 1 and there(u - 1):
                        dve.wait_ge(c_pv, 2 + PAIRS * u)
                        nc.vector.tensor_copy(att_t[:], bank[6]).then_inc(c_oe, 1)
                    if i == 6 and there(u - 1):
                        add_attended(u - 1, (j - 1) % 8)
                    if j == 1 and i % 2 == 1 and there(u - 1 - KVH):
                        at, st = u - 1 - KVH, i // 2
                        c.inc(nc.vector.bn_stats(st6_all[:, bass.ds(at * (6 * ST // KVH) + 6 * st, 6)],
                                                 X[:, bass.ds(at * (ST * D // KVH) + st * D, D)]))
                    if there(m):
                        for g in (2 * i, 2 * i + 1):
                            h, st = g // ST, g % ST
                            dve.wait_ge(c_mx, 16 * m + g + 1)
                            nc.vector.tensor_reduce(neg_max[mj % 2][:, st * GROUP + h:st * GROUP + h + 1], bank[g % 2],
                                                    AX.X, ALU.max, negate=True).then_inc(c_red, 1)
                if there(m):
                    qs = q_s[mj % 4][:].rearrange("p (n c) -> p n c", c=64)
                    nm = neg_max[mj % 2][:].rearrange("p (n c) -> p n c", c=1)
                    dve.wait_ge(c_red, 2 + 16 * (m + 1))
                    dve.wait_ge(c_prep, 3 * (m + 1))
                    c.step(nc.vector.tensor_copy(qs[:, :, 48:49], nm))
                    nc.vector.tensor_tensor(qs[:, :, 49:50], nm, qs[:, :, 48:49], ALU.subtract).then_inc(c_m, 1)

            def phase_d():
                c.wait()
                for t in range(TILES):
                    c.inc(nc.vector.bn_aggr(mv_all[:, 2 * t:2 * t + 2], st6_all[:, 6 * t:6 * t + 6]))
                c.wait()
                nc.vector.tensor_scalar(ve_all[:], mv_all[:, 1:2 * TILES:2], 1.0, EPS_LN, ALU.mult, ALU.add).then_inc(c_var, 1)
                dve.wait_ge(c_rstd, 2)
                for t in range(TILES):
                    nc.vector.tensor_scalar(xn[:, t * D:(t + 1) * D], X[:, t * D:(t + 1) * D], mv_all[:, 2 * t:2 * t + 1],
                                            rstd_all[:, t:t + 1], ALU.subtract, ALU.mult).then_inc(d_xn, 1)
                dve.wait_ge(d_lg, TILES)
                c.step(nc.vector.tensor_copy(lg[:], bank[0][:, 0:TILES * EXPERTS]))
                for t in range(TILES):
                    s = slice(t * EXPERTS, (t + 1) * EXPERTS)
                    c.inc(nc.vector.max(top[:, s], lg[:, s]))
                c.wait()

                def by_tile(a, e=EXPERTS):
                    return a.rearrange("p (t e) -> p t e", e=e)

                dve.wait_ge(ld_d, 4 * 16)
                top3 = by_tile(top[:])
                nc.vector.tensor_tensor(by_tile(gap[:], 1), top3[:, :, 1:2], top3[:, :, 0:1], ALU.subtract).then_inc(d_gap, 1)
                for k in range(2):
                    largest = top3[:, :, k:k + 1].broadcast_to([P, TILES, EXPERTS])
                    c.step(nc.vector.tensor_tensor(by_tile(picked[k][:]), by_tile(lg[:]), largest, ALU.is_equal))
                    c.step(nc.vector.tensor_tensor(picked[k][:], picked[k][:], num_e[:], ALU.mult))
                    if k == 1:
                        c.step(nc.vector.tensor_tensor(both[:], picked[1][:], chosen[0][:], ALU.mult))
                        c.step(nc.vector.tensor_tensor(picked[1][:], picked[1][:], both[:], ALU.subtract))
                    c.step(nc.vector.tensor_reduce(by_tile(slot_f[k][:], 1), by_tile(picked[k][:]), AX.X, ALU.max))
                    number = by_tile(slot_f[k][:], 1).broadcast_to([P, TILES, EXPERTS])
                    c.step(nc.vector.tensor_tensor(by_tile(chosen[k][:]), by_tile(num_e[:]), number, ALU.is_equal))
                nc.vector.tensor_tensor(both[:], chosen[0][:], chosen[1][:], ALU.add).then_inc(d_both, 1)
                c.inc(nc.vector.memset(running[:, 0:EXPERTS], 0.0))
                n = TILES * EXPERTS
                dve.wait_ge(d_rank, 1)
                for t in range(TILES):
                    c.wait()
                    s = slice(t * EXPERTS, (t + 1) * EXPERTS)
                    c.inc(nc.vector.tensor_tensor(running[:, (t + 1) * EXPERTS:(t + 2) * EXPERTS], running[:, s],
                                                  bank[1][:, n + t * EXPERTS:n + (t + 1) * EXPERTS], ALU.add))
                c.wait()
                c.step(nc.vector.tensor_tensor(slot_e[:], running[:, 0:n], bank[1][:, 0:n], ALU.add))
                count = running[:, n:n + EXPERTS]
                c.step(nc.vector.tensor_scalar(row8_i["count"][:], count, float(P - 1), None, ALU.add))
                c.step(nc.vector.tensor_scalar(row8_i["tiles"][:], row8_i["count"][:], 7, None, ALU.logical_shift_right))
                c.step(nc.vector.tensor_copy(row8["tiles"][:], row8_i["tiles"][:]))
                c.step(nc.vector.tensor_copy(row8["end"][:, 0:1], row8["tiles"][:, 0:1]))
                for e in range(1, EXPERTS):
                    c.step(nc.vector.tensor_tensor(row8["end"][:, e:e + 1], row8["end"][:, e - 1:e], row8["tiles"][:, e:e + 1], ALU.add))
                c.step(nc.vector.tensor_tensor(row8["first"][:], row8["end"][:], row8["tiles"][:], ALU.subtract))
                c.step(nc.vector.tensor_scalar(row8["first"][:], row8["first"][:], float(P), None, ALU.mult))
                c.step(nc.vector.tensor_tensor(by_tile(slot_e[:]), by_tile(slot_e[:]),
                                               row8["first"][:].rearrange("p (t e) -> p t e", t=1).broadcast_to([P, TILES, EXPERTS]), ALU.add))
                for k in range(2):
                    c.step(nc.vector.tensor_tensor(picked[k][:], slot_e[:], chosen[k][:], ALU.mult))
                    c.step(nc.vector.tensor_reduce(by_tile(slot_f[k][:], 1), by_tile(picked[k][:]), AX.X, ALU.add))
                    nc.vector.tensor_copy(slot[k][:], slot_f[k][:]).then_inc(d_slot, 1)
                plan_tiles()
                dve.wait_ge(d_gap_e, 1)
                c.step(nc.vector.tensor_scalar(gap_1[:], gap_e[:], 1.0, None, ALU.add))
                c.step(nc.vector.reciprocal(top_w[0][:], gap_1[:]))
                c.step(nc.vector.tensor_tensor(top_w[1][:], gap_e[:], top_w[0][:], ALU.mult))

                def step(i, parity):
                    for half in range(2):
                        dve.wait_ge(e_silu, 2 * i + half + 1)
                        h = h_d[:, half * 512:(half + 1) * 512]
                        nc.vector.tensor_tensor(h, bank[2 * half + 1], h, ALU.mult).then_inc(e_h, 1)
                    if not static(i) or i + 1 < MTILES:
                        x_second(i + 1)
                    if not static(i) or i > 0:
                        move_y(i - 1, 1 - parity)
                    for half in range(2):
                        dve.wait_ge(e_hh, 2 * i + half + 1)
                        s = slice(half * 512, (half + 1) * 512)
                        nc.vector.tensor_tensor(h_lo_d[:, s], bank[5 + half], h_hi_d[:, s], ALU.subtract).then_inc(e_hl, 1)

                def x_second(i):
                    dve.wait_ge(e_xh, i + 1)
                    nc.vector.tensor_tensor(x_lo[:], bank[4], x_hi[:], ALU.subtract).then_inc(e_xl, 1)

                def move_y(i, parity):
                    dve.wait_ge(e_wo, i + 2)
                    if not (static(i) and i < 2):
                        dve.wait_ge(e_st[parity], 8 * (i - parity))
                    nc.vector.tensor_copy(y_out[parity][:], bank[7]).then_inc(e_y, 1)

                x_second(0)
                tile_loop(dve, step)
                move_y(MTILES - 1, 0)
                dve.wait_ge(x_back, 16)
                for t in range(TILES):
                    xt = X2[:, t * D:(t + 1) * D]
                    dve.wait_ge(d_got[t % 8], 32 * (t // 8 + 1))
                    for k in range(2):
                        nc.vector.scalar_tensor_tensor(out=xt, in0=xn[:, (2 * t + k) % 16 * D:((2 * t + k) % 16 + 1) * D],
                                                       scalar=top_w[k][:, t:t + 1], in1=xt, op0=ALU.mult,
                                                       op1=ALU.add).then_inc(d_out, 1)
                        dve.wait_ge(d_out, 2 * t + k + 1)

            def plan_tiles():
                def by_mt(a, e=EXPERTS):
                    return a.rearrange("p (t e) -> p t e", e=e)

                def over_tiles(a):
                    return a.rearrange("p (t e) -> p t e", t=1).broadcast_to([1, MTILES, EXPERTS])

                c.inc(nc.vector.tensor_scalar(row8_i["wait"][0:1, :], row8["end"][0:1, :], 1.0, None, ALU.add))
                num = by_mt(num_tile[:])
                c.step(nc.vector.tensor_tensor(by_mt(past_end[:]), num, over_tiles(row8["end"][0:1, :]), ALU.is_ge))
                c.step(nc.vector.tensor_reduce(by_mt(mt["expert"][:], 1), by_mt(past_end[:]), AX.X, ALU.add))
                plan3 = plan[:].rearrange("p (t c) -> p t c", c=3)
                c.step(nc.vector.tensor_scalar(mt["expert"][:], mt["expert"][:], float(EXPERTS - 1), None, ALU.min))
                c.step(nc.vector.tensor_copy(mt_i["expert"][:], mt["expert"][:]))
                c.step(nc.vector.tensor_scalar(mt_i["half"][:], mt_i["expert"][:], 1, None, ALU.logical_shift_right))
                c.step(nc.vector.tensor_copy(mt["half"][:], mt_i["half"][:]))
                c.step(nc.vector.scalar_tensor_tensor(out=mt["parity"][:], in0=mt["half"][:], scalar=-2.0, in1=mt["expert"][:],
                                                      op0=ALU.mult, op1=ALU.add))
                for i in range(2):
                    c.step(nc.vector.tensor_scalar(plan3[:, :, i:i + 1], by_mt(mt["parity"][:], 1), float(W_IN[1][i] - W_IN[0][i]),
                                                   float(W_IN[0][i]), ALU.mult, ALU.add))
                nc.vector.tensor_scalar(plan3[:, :, 2:3], by_mt(mt["expert"][:], 1), 2.0, 1.0, ALU.mult, ALU.add).then_inc(d_plan, 1)

            def add_attended(v, vj):
                dve.wait_ge(c_to, v + 1)
                o = bank[7].rearrange("p (n c) -> p n c", c=32)
                c.step(nc.vector.reciprocal(att_r[:].rearrange("p (n c) -> p n c", c=1), o[:, :, HD:HD + 1]))
                nc.vector.tensor_tensor(att_n[:].rearrange("p (n c) -> p n c", c=HD), o[:, :, 0:HD],
                                        att_r[:].rearrange("p (n c) -> p n c", c=1).broadcast_to([P, ST * GROUP, HD]),
                                        ALU.mult).then_inc(c_eo, 1)
                dve.wait_ge(c_eo, v + 1)
                xs = x_unit(v, vj)
                nc.vector.tensor_tensor(xs, xs, att_n[:].rearrange("p (t c) -> p t c", t=ST), ALU.add).then_inc(c_x, 1)
                dve.wait_ge(c_x, v + 1)

            def x_unit(v, vj):
                at = (v - vj) * (ST * D // KVH)
                return X[:, bass.ds(at, ST * D)].rearrange("p (t c) -> p t c", c=D)[:, :, vj * 64:(vj + 1) * 64]

            def phase_c():
                c.wait()
                for t in range(TILES):
                    c.inc(nc.vector.bn_aggr(mv_all[:, 2 * t:2 * t + 2], st6_all[:, 6 * t:6 * t + 6]))
                c.wait()
                nc.vector.tensor_scalar(ve_all[:], mv_all[:, 1:2 * TILES:2], 1.0, EPS_LN, ALU.mult, ALU.add).then_inc(c_var, 1)
                for parts in q_s + k_s:
                    nc.vector.memset(parts[:].bitcast(F32), 0.0).then_inc(c_zero, 1)
                for i in range(4):
                    nc.vector.memset(k_lo[i][64:P, :].bitcast(F32), 0.0).then_inc(c_zero, 1)
                    nc.vector.memset(k_hi[i][0:64, :].bitcast(F32), 0.0).then_inc(c_zero, 1)
                slots(dve, attention, c, 2 * KVH + ST)
            dve.sem_inc(b_g, 2)
            dve.sem_inc(b_y, 2)
            dve.sem_inc(b_q2, 1)
            dve.wait_ge(ld_x, 16)
            dve.wait_ge(pool_const, 3)
            dve.wait_ge(ld_const, 5 * 16)
            layer_norm(0, a_p, 1, a_normed)
            for b in range(BATCH):
                phase_a(b)
            dve.wait_ge(had_ready, 1)
            layer_norm(0, h_n, 2 * BATCH + 1, b_normed)
            with dve.Fori(0, BATCH - 1) as b:
                c.enter(b, 2 * ST + 1 + ST + 4 + 5 * ST)
                phase_b(b, True)
                c.leave(BATCH - 1)
            phase_b(BATCH - 1, False)
            dve.sem_inc(c_red, 2)
            dve.sem_inc(c_oe, 1)
            phase_c()
            dve.sem_inc(e_h, 2)
            dve.sem_inc(e_y, 1)
            phase_d()

        @block.tensor
        def _(pe):
            def context_t():
                pe.wait_ge(ld_ctx, 16)
                for b in range(BATCH):
                    for t in range(ST):
                        last = nc.tensor.transpose(bank[b][:, t * P:(t + 1) * P],
                                                   ctx_raw[:, (b * ST + t) * CTX:(b * ST + t + 1) * CTX], ident[:])
                    last.then_inc(ctx_t_ps, 1)
                nc.tensor.transpose(bank[4][:, 0:CTX], wk_sb[:], ident[:]).then_inc(ctx_t_ps, 1)

            def phase_a(b):
                nc.tensor.matmul(bank[2], wk_t[:], ctx_t[:, bass.ds(b * SEQ, SEQ)], start=True, stop=True).then_inc(a_kvt, 1)
                for st in range(ST):
                    pe.wait_ge(a_normed, b * ST + st + 1)
                    if st >= 2:
                        pe.wait_ge(a_trans_sb, b * ST + st - 1)
                    for k in range(DC):
                        last = nc.tensor.transpose(bank[st % 2][:, k * P:(k + 1) * P],
                                                   a_p[:, st * D + k * P:st * D + (k + 1) * P], ident[:])
                    last.then_inc(a_trans, 1)
                weight_rows(b, 0, 2)
                pe.wait_ge(a_kvt_sb, b + 1)
                for t in range(ST):
                    last = nc.tensor.transpose(bank[2][:, t * CTX:(t + 1) * CTX], kv_t[:, t * P:(t + 1) * P], ident[:])
                last.then_inc(a_kv, 1)
                weight_rows(b, 2, 4)
                pe.wait_ge(a_kv_sb, b + 1)
                pe.wait_ge(a_trans_sb, b * ST + ST)
                for k in range(DC):
                    last = nc.tensor.matmul(bank[2], kv[:, k * CTX:(k + 1) * CTX], a_pt[:, k * SEQ:(k + 1) * SEQ],
                                            start=(k == 0), stop=(k == DC - 1))
                last.then_inc(a_out, 1)
                weight_rows(b, 4, 6)
                pe.wait_ge(a_out_sb, b + 1)
                for st in range(ST):
                    nc.tensor.matmul(bank[4 + st], o_t[:, st * P:(st + 1) * P], kv_t[:], start=True,
                                     stop=True).then_inc(a_sim, 1)

                weight_rows(b, 6, FC)
                if b < 3:
                    pe.wait_ge(w_abs, b + 1)
                    if b:
                        pe.wait_ge(w_evac, b * FC)
                    nc.tensor.matmul(bank[3][:, b:b + 1], ones[:], abs_sum[:, b:b + 1], start=True, stop=True).then_inc(w_tot, 1)

            def weight_rows(b, start, end):
                for u in range(start, end if b else start):
                    unit = (b - 1) * FC + u
                    pe.wait_ge(w_tern, unit + 1)
                    if unit:
                        pe.wait_ge(w_evac, unit)
                    for j in range(4):
                        last = nc.tensor.transpose(bank_b[3][:, j * P:(j + 1) * P], tern[u % 2][:, j * P:(j + 1) * P], ident_b[:])
                    last.then_inc(w_tp, 1)

            def phase_b(b):
                def rotate(st):
                    pe.wait_ge(b_lo, b * ST + st + 1)
                    for k in range(DC):
                        for part, h in enumerate((h_hi, h_lo)):
                            last = nc.tensor.matmul(bank[4 + st], h[:, st * D + k * P:st * D + (k + 1) * P], had[:, k * D:(k + 1) * D],
                                                    start=(k + part == 0), stop=(k + part == DC))
                    last.then_inc(b_fw, 1)

                for st in range(ST):
                    pe.wait_ge(b_normed, b * ST + st + 1)
                    if st >= 2:
                        pe.wait_ge(b_lo, b * ST + st - 1)
                    for k in range(DC):
                        last = nc.tensor.transpose(bank[st % 2][:, k * P:(k + 1) * P],
                                                   h_n[:, st * D + k * P:st * D + (k + 1) * P], ident[:])
                    last.then_inc(b_trans, 1)
                    if st > 0:
                        rotate(st - 1)
                rotate(ST - 1)
                pe.wait_ge(b_dg, b + 1)
                for st in range(ST):
                    last = nc.tensor.matmul(bank[0][:, st * P:(st + 1) * P], ones[:], diag[:, st * P:(st + 1) * P], start=True, stop=True)
                last.then_inc(b_sps, 1)
                for st in range(ST):
                    pe.wait_ge(b_q, b * ST + st + 1)
                    if st >= 2:
                        pe.wait_ge(b_qts, b * ST + st - 1)
                    for k in range(DC):
                        last = nc.tensor.transpose(bank_b[2 + st % 2][:, k * P:(k + 1) * P],
                                                   q_b[:, st * D + k * P:st * D + (k + 1) * P], ident_b[:])
                    last.then_inc(b_qt, 1)
                for a in range(2):
                    with pe.Fori(0, 4) as i:
                        n = b * FC + a * 8 + 2 * i
                        pe.wait_ge(b_qts, b * ST + ST)
                        pe.wait_ge(b_sbc, b + 1)
                        for w, (freed, ready) in enumerate(((b_g, b_gp), (b_y, b_up))):
                            for h in range(2):
                                pe.wait_ge(freed, n + h + 1)
                                for k in range(DC):
                                    last = nc.tensor.matmul(bank[2 * w + h], wgu_t[w][:, bass.ds(k * FF + (8 * a + i + 4 * h) * P, P)],
                                                            q_t[:, k * SEQ:(k + 1) * SEQ], start=(k == 0), stop=(k == DC - 1))
                                last.then_inc(ready, 1)
                pe.wait_ge(b_y, 2 + (b + 1) * FC)

                def quantised_transposed(n):
                    pe.wait_ge(b_q2, 1 + n)
                    for j in range(FC):
                        last = nc.tensor.transpose(bank_b[j // 8][:, (j % 8) * P:(j % 8 + 1) * P],
                                                   q_b[:, j * P:(j + 1) * P], ident_b[:])
                    last.then_inc(b_tr, 1)

                for st in range(ST + 1):
                    n = b * ST + st
                    if st < ST:
                        if st > 0:
                            pe.wait_ge(b_zlo, (ST - 1) * b + st)
                        for g in range(4):
                            if st == 0 and g % 2 == 0:
                                pe.wait_ge(b_zlo0, 2 * b + g // 2 + 1)
                            if g == 3 and st > 0:
                                quantised_transposed(n)
                            pe.wait_ge(b_zc, 4 * n + g + 1)
                            for k in range(DC):
                                at = (g * DC + k) * SEQ + st * P
                                for part, y in enumerate((Z_hi, Y_lo)):
                                    last = nc.tensor.matmul(bank[4 + g], y[:, at:at + P], had[:, k * D:(k + 1) * D],
                                                            start=(k + part == 0), stop=(k + part == DC))
                            last.then_inc(b_z, 1)
                    if st == ST:
                        quantised_transposed(n)
                    if st > 0:
                        pe.wait_ge(b_q2ts, n)
                        if st > 2:
                            pe.wait_ge(b_x, n - 2)
                        for j in range(FC):
                            last = nc.tensor.matmul(bank[2 + (st - 1) % 2], q2_t[:, j * P:(j + 1) * P], wd_t[:, j * D:(j + 1) * D],
                                                    start=(j == 0), stop=(j == FC - 1))
                        last.then_inc(b_dn, 1)

            free = []

            def bank_job(ready, inputs, done, freed):
                for s_, v_ in ready + free:
                    pe.wait_ge(s_, v_)
                for t, a in enumerate(inputs):
                    last = nc.tensor.transpose(bank[7][:, t * P:(t + 1) * P], a, ident[:])
                last.then_inc(done, 1)
                free[:] = [freed]

            def query_inputs(mj, p):
                q = q_s[mj % 4][:].bitcast(F32)
                return [q[:, (t * GROUP + 2 * p) * 64:(t * GROUP + 2 * p + 2) * 64] for t in range(ST)]

            def key_job(v, vj):
                k = k_s[vj % 2][:].bitcast(F32)
                bank_job([(c_prep, 3 * (v + 1))], [k[:, t * P:(t + 1) * P] for t in range(ST)], c_tk, (c_ek, 2 * (v + 1)))

            def attention(u, j, there):
                m, mj = u + 2, (j + 2) % 8

                def attend(n, i, vj):
                    t, p = i // 2, i % 2
                    pe.wait_ge(c_e, 2 + n + 1)
                    for h in range(2):
                        last = nc.tensor.matmul(bank[6][(2 * p + h) * 32:(2 * p + h + 1) * 32, :], v_u[vj % 8][:, t * 32:(t + 1) * 32],
                                                prob[i % 2][:, h * SEQ:(h + 1) * SEQ], start=(t == 0), stop=(t == ST - 1))
                    last.then_inc(c_pv, 1)

                def maxima(g):
                    if there(m):
                        h, st = g // ST, g % ST
                        if g in (0, 8):
                            pe.wait_ge(c_eqm, 2 * m + g // 8 + 1)
                            pe.wait_ge(c_ek, 2 * (m + 1))
                        pe.wait_ge(c_red, 16 * m + g + 1)
                        nc.tensor.matmul(bank[g % 2], q_m[h // 2][:, st * P:(st + 1) * P],
                                         (k_lo, k_hi)[h % 2][mj % 4][:], start=True, stop=True).then_inc(c_mx, 1)

                if there(m):
                    free[:] = [(c_eqm, 2 * m + 2)]
                for i in range(PAIRS):
                    if i in (1, 2) and there(m - 1):
                        v, p = m - 1, i - 1
                        bank_job([(c_m, v + 1)], query_inputs(mj - 1, p), c_tqe, (c_eqe, 2 * v + p + 1))
                    if i == 3 and there(m + 1):
                        key_job(m + 1, mj + 1)
                    if i == 4 and there(m + 1):
                        bank_job([], query_inputs(mj + 1, 0), c_tqm, (c_eqm, 2 * (m + 1) + 1))
                    if i == 5 and there(u - 1):
                        bank_job([(c_oe, 1 + u)], [att_t[:, t * P:(t + 1) * P] for t in range(ST)], c_to, (c_eo, u))
                    if i == 7 and there(m + 1):
                        bank_job([], query_inputs(mj + 1, 1), c_tqm, (c_eqm, 2 * (m + 1) + 2))
                    maxima(2 * i)
                    if there(u):
                        n = PAIRS * u + i
                        t, p = i // 2, i % 2
                        if i < 2:
                            pe.wait_ge(c_eqe, 2 * u + p + 1)
                        pe.wait_ge(c_e, n + 1)
                        for h in range(2):
                            last = nc.tensor.matmul(bank[2 + 2 * (i % 2) + h], (k_lo, k_hi)[h][j % 4][:, t * P:(t + 1) * P],
                                                    q_e[j % 2][p][:], start=True, stop=True)
                        last.then_inc(c_s, 1)
                    maxima(2 * i + 1)
                    if i == 0 and there(u - 1):
                        attend(PAIRS * u - 1, PAIRS - 1, j - 1)
                    if i > 0 and there(u):
                        if i == 1:
                            pe.wait_ge(c_oe, u + 1)
                        attend(PAIRS * u + i - 1, i - 1, j)

            def phase_c():
                pe.wait_ge(c_const, 19)
                pe.wait_ge(c_zero, 6 + 8)
                key_job(0, 0)
                for p in range(2):
                    bank_job([], query_inputs(0, p), c_tqm, (c_eqm, p + 1))
                slots(pe, attention)

            def phase_d():
                def logits(t):
                    pe.wait_ge(d_trs, t + 1)
                    for k in range(DC):
                        last = nc.tensor.matmul(bank[0][:, t * EXPERTS:(t + 1) * EXPERTS], xn_t[t % 4][:, k * P:(k + 1) * P],
                                                gw[:, k * EXPERTS:(k + 1) * EXPERTS], start=(k == 0), stop=(k == DC - 1))
                    last.then_inc(d_lg, 1)

                pe.wait_ge(ld_d, 4 * 16)
                for t in range(TILES):
                    pe.wait_ge(d_xn, t + 1)
                    if t >= 4:
                        pe.wait_ge(d_trs, t - 3)
                    for k in range(DC):
                        last = nc.tensor.transpose(bank[2 + t % 4][:, k * P:(k + 1) * P],
                                                   xn[:, t * D + k * P:t * D + (k + 1) * P], ident[:])
                    last.then_inc(d_tr, 1)
                    if t >= 2:
                        logits(t - 2)
                logits(TILES - 2)
                logits(TILES - 1)
                pe.wait_ge(d_both, 1)
                n = TILES * EXPERTS
                nc.tensor.matmul(bank[1][:, 0:n], before[:], both[:], start=True, stop=True)
                nc.tensor.matmul(bank[1][:, n:2 * n], ones[:], both[:], start=True, stop=True).then_inc(d_rank, 1)

                def transpose_x(i, parity):
                    pe.wait_ge(e_ld[parity], 8 * (i - parity) + 16)
                    for k in range(DC):
                        last = nc.tensor.transpose(bank[4][:, k * P:(k + 1) * P], x_in[parity][:, k * P:(k + 1) * P], ident[:])
                    last.then_inc(e_xtr, 1)

                def down(i):
                    first_step = first_of_expert(i)
                    pe.wait_ge(e_hl, 2 * i + 2)
                    pe.wait_ge(e_y, i + 1)
                    for k in range(MOE // P):
                        if k % 4 == 0:
                            pe.wait_ge(wo_parts, first_step + k // 4)
                        last = products(bank[7], h_hi_d, h_lo_d, k * P, WO + k * D, k == 0, k == MOE // P - 1)
                    last.then_inc(e_wo, 1)

                def first_of_expert(i):
                    return pe.value_load(plan[0:1, bass.ds(3 * i + 2, 1)], min_val=1, max_val=2 * EXPERTS - 1)

                def products(out_bank, hi, lo, at, w_at, start, stop):
                    cols = slice(at, at + P)
                    nc.tensor.matmul(out_bank, hi[:, cols], w_r[:, bass.ds(w_at, 512)], start=start, stop=False)
                    nc.tensor.matmul(out_bank, hi[:, cols], w_r[:, bass.ds(w_at + BLOCK, 512)], start=False, stop=False)
                    return nc.tensor.matmul(out_bank, lo[:, cols], w_r[:, bass.ds(w_at, 512)], start=False, stop=stop)

                def step(i, parity):
                    at = [pe.value_load(plan[0:1, bass.ds(3 * i + w, 1)], min_val=0, max_val=max(W_IN[0][w], W_IN[1][w]))
                          for w in range(2)]
                    first_step = first_of_expert(i)
                    pe.wait_ge(e_xl, i + 1)
                    for half in range(2):
                        pe.wait_ge(e_h, 2 * i + half + 1)
                        for w in range(2):
                            if half == 0:
                                pe.wait_ge(w_in_parts, first_step + w)
                            for k in range(DC):
                                last = products(bank[2 * half + w], x_hi, x_lo, k * P, at[w] + k * MOE + half * 512, k == 0, k == DC - 1)
                        last.then_inc(e_gu, 1)
                    if not static(i) or i + 1 < MTILES:
                        transpose_x(i + 1, 1 - parity)
                    if not static(i) or i > 0:
                        down(i - 1)
                    for half in range(2):
                        pe.wait_ge(e_h, 2 * i + half + 3)
                        for k in range(4):
                            last = nc.tensor.transpose(bank[5 + half][:, k * P:(k + 1) * P],
                                                       h_d[:, (4 * half + k) * P:(4 * half + k + 1) * P], ident[:])
                        last.then_inc(e_htr, 1)

                pe.wait_ge(d_plan, 1)
                transpose_x(0, 0)
                tile_loop(pe, step)
                down(MTILES - 1)

            pe.sem_inc(e_xtr, 2)
            pe.sem_inc(e_wo, 1)
            pe.sem_inc(e_htr, 2)
            pe.sem_inc(w_tp, 2)
            pe.sem_inc(b_tr, 1)
            pe.sem_inc(b_zc, 4)
            pe.sem_inc(c_tqe, 8)
            pe.sem_inc(c_tk, 2)
            pe.sem_inc(c_pv, 2)
            pe.wait_ge(ld_const, 5 * 16)
            context_t()
            pe.wait_ge(ctx_t_sb, BATCH + 1)
            pe.wait_ge(pool_const, 4)
            for b in range(BATCH):
                phase_a(b)
            pe.wait_ge(had_ready, 1)
            with pe.Fori(0, BATCH) as b:
                phase_b(b)
            phase_c()
            phase_d()


def constants():
    h = np.ones((1, 1), np.float32)
    while h.shape[0] < D:
        h = np.block([[h, h], [h, -h]]).astype(np.float32)
    hadamard = h.reshape(DC, P, D).transpose(1, 0, 2).reshape(P, DC * D)
    before = np.triu(np.ones((P, P), np.float32), 1)
    routing = np.zeros((2, 512), np.float32)
    routing[0, :TILES * EXPERTS] = np.tile(EXPERTS - np.arange(EXPERTS), TILES)
    routing[1, :MTILES * EXPERTS] = np.repeat(np.arange(MTILES), EXPERTS)
    return {"c_ident": np.eye(P, dtype=np.float32), "c_hadamard": np.ascontiguousarray(hadamard, np.float32),
            "c_before": before, "c_routing": routing}


_INS = ["x", "ctx_512", "L0_xattn_W_k", "L0_xattn_b_k", "L0_xattn_ln_gamma", "L0_xattn_ln_beta", "L0_ffn_w_gate",
        "L0_ffn_w_up", "L0_ffn_w_down", "L1_ffn_gate_w", "L1_ffn_w0", "L1_ffn_w1", "L1_ffn_wo"]


def kernel(**inputs):
    import concourse.bacc as bacc
    from concourse.bass_utils import run_bass_kernel_spmd

    nc = bacc.Bacc("TRN2", target_bir_lowering=False, num_devices=1)
    arrays, args = {}, []
    for name, a in [(n, inputs[n]) for n in _INS] + list(constants().items()):
        a = np.ascontiguousarray(a)
        arrays[f"in_{name}"] = a
        args.append(nc.dram_tensor(f"in_{name}", a.shape, mybir.dt.from_np(a.dtype), kind="ExternalInput").ap())
    args.append(nc.dram_tensor("out", (BATCH, SEQ, D), F32, kind="ExternalOutput").ap())
    network(nc, *args)
    result = run_bass_kernel_spmd(nc, [arrays], core_ids=[0])
    return result.results[0]["out"]
```
